# Optimizing a Trainium2 kernel written in Bass

```python
import numpy as np
import jax
import jax.numpy as jnp

def _softmax(x, axis=-1):
    return jax.nn.softmax(x, axis=axis)

def _gelu(x):
    return jax.nn.gelu(x, approximate=True)

def _silu(x):
    return jax.nn.silu(x)

def _sigmoid(x):
    return jax.nn.sigmoid(x)

def _layernorm(x, axis=-1, eps=1e-05):
    m = jnp.mean(x, axis=axis, keepdims=True)
    v = jnp.var(x, axis=axis, keepdims=True)
    return (x - m) / jnp.sqrt(v + eps)

def _scatter_add(tgt, idx, src, axis=0):
    return tgt.at[idx].add(src)

def _segment_sum(src, seg, n):
    return jax.ops.segment_sum(src, seg, n)
kernel_name = 'mk_gnn_resnorm_d2_gnn_r8_43d098'

def setup_inputs(seed: int=0):
    np.random.seed(seed)
    _w = jnp.asarray

    def _rec_inputs():
        import jax
        import jax.numpy as jnp
        _gk = jax.random.key(seed)
        x = -0.000202 + 1 * jax.random.normal(jax.random.fold_in(_gk, 1), (6250, 128), jnp.float32)
        src = jax.random.randint(jax.random.fold_in(_gk, 2), (100000,), 0, 6250, jnp.int32)
        dst = jnp.minimum((6250 * jax.random.uniform(jax.random.fold_in(_gk, 3), (100000,)) ** 2.0).astype(jnp.int32), 49999)
        _o = jnp.argsort(dst, stable=True)
        src = src[_o]
        dst = dst[_o]
        edge_attr_64 = 1.36993e-05 + 0.999972 * jax.random.normal(jax.random.fold_in(_gk, 12), (100000, 64), jnp.float32)
        edge_weight = jax.random.uniform(jax.random.fold_in(_gk, 13), (100000,), jnp.float32, 0.0, 1)
        return (x, src, dst, edge_attr_64, edge_weight)
    x, src, dst, edge_attr_64, edge_weight = _rec_inputs()

    def _L0_gnn_setup():
        import jax, jax.numpy as jnp
        import numpy as np
        N_NODES = 6250
        N_EDGES = 100000
        HID = 128
        key = jax.random.key(seed)
        ks = jax.random.split(key, 10)
        s_msg = 1.0 / np.sqrt(2 * HID + 1)
        s_u1 = 1.0 / np.sqrt(2 * HID)
        s_u2 = 1.0 / np.sqrt(HID)
        return {'z': jax.random.normal(ks[0], (N_NODES, HID), dtype=jnp.float32), 'edge_weight': jax.random.uniform(ks[1], (N_EDGES,), dtype=jnp.float32), 'edge_src': jax.random.randint(ks[2], (N_EDGES,), 0, N_NODES), 'edge_dst': jax.random.randint(ks[3], (N_EDGES,), 0, N_NODES), 'Wm': jax.random.normal(ks[4], (2 * HID + 1, HID), dtype=jnp.float32) * s_msg, 'bm': jax.random.normal(ks[5], (HID,), dtype=jnp.float32) * s_msg, 'W1': jax.random.normal(ks[6], (2 * HID, HID), dtype=jnp.float32) * s_u1, 'b1': jax.random.normal(ks[7], (HID,), dtype=jnp.float32) * s_u1, 'W2': jax.random.normal(ks[8], (HID, HID), dtype=jnp.float32) * s_u2, 'b2': jax.random.normal(ks[9], (HID,), dtype=jnp.float32) * s_u2}
    _L0_gnn_all = _L0_gnn_setup()
    _L0_gnn_in = {k: v for k, v in _L0_gnn_all.items() if k in ('Wm', 'bm', 'W1', 'b1', 'W2', 'b2')}
    del _L0_gnn_all

    def _L1_gnn_setup():
        import jax, jax.numpy as jnp
        import numpy as np
        N, E, D, DE, M, K = (2500, 40000, 128, 64, 3, 3)

        def _seg_softmax(x, seg, n):
            m = jax.ops.segment_max(x, seg, num_segments=n)
            e = jnp.exp(x - m[seg])
            z = jax.ops.segment_sum(e, seg, num_segments=n)
            return e / z[seg]
        key = jax.random.key(seed)
        ks = jax.random.split(key, 16)
        s = 0.05
        return {'node_features': jax.random.normal(ks[0], (N, D), jnp.float32), 'edge_features': jax.random.normal(ks[1], (E, DE), jnp.float32), 'src': jax.random.randint(ks[2], (E,), 0, N, jnp.int32), 'dst': jax.random.randint(ks[3], (E,), 0, N, jnp.int32), 'node_att_W': jax.random.normal(ks[4], (K, D, D), jnp.float32) * s, 'rel_att_W': jax.random.normal(ks[5], (M, D, D), jnp.float32) * s, 'rel_att_W1': jax.random.normal(ks[6], (M, DE, D), jnp.float32) * s, 'rel_att_b1': jax.random.normal(ks[7], (M, D), jnp.float32) * s, 'rel_att_W2': jax.random.normal(ks[8], (M, D), jnp.float32) * s, 'rel_att_b2': jax.random.normal(ks[9], (M,), jnp.float32) * s, 'node_fc_W': jax.random.normal(ks[10], (D, D), jnp.float32) * s, 'node_fc_b': jnp.zeros((D,), jnp.float32), 'edge_fc_W': jax.random.normal(ks[11], (DE, DE), jnp.float32) * s, 'edge_fc_b': jnp.zeros((DE,), jnp.float32), 'out_fc_W': jax.random.normal(ks[12], (2 * D, D), jnp.float32) * s, 'out_fc_b': jnp.zeros((D,), jnp.float32), 'gate_W': jax.random.normal(ks[13], (D, 1), jnp.float32) * s, 'gate_b': jnp.zeros((1,), jnp.float32)}
    _L1_gnn_all = _L1_gnn_setup()
    _L1_gnn_in = {k: v for k, v in _L1_gnn_all.items() if k in ('node_att_W', 'rel_att_W', 'rel_att_W1', 'rel_att_b1', 'rel_att_W2', 'rel_att_b2', 'node_fc_W', 'node_fc_b', 'edge_fc_W', 'edge_fc_b', 'out_fc_W', 'out_fc_b', 'gate_W', 'gate_b')}
    del _L1_gnn_all
    return {'x': x, 'src': src, 'dst': dst, 'edge_attr_64': edge_attr_64, 'edge_weight': edge_weight, 'L0_gnn_Wm': _L0_gnn_in['Wm'], 'L0_gnn_bm': _L0_gnn_in['bm'], 'L0_gnn_W1': _L0_gnn_in['W1'], 'L0_gnn_b1': _L0_gnn_in['b1'], 'L0_gnn_W2': _L0_gnn_in['W2'], 'L0_gnn_b2': _L0_gnn_in['b2'], 'L1_gnn_node_att_W': _L1_gnn_in['node_att_W'], 'L1_gnn_rel_att_W': _L1_gnn_in['rel_att_W'], 'L1_gnn_rel_att_W1': _L1_gnn_in['rel_att_W1'], 'L1_gnn_rel_att_b1': _L1_gnn_in['rel_att_b1'], 'L1_gnn_rel_att_W2': _L1_gnn_in['rel_att_W2'], 'L1_gnn_rel_att_b2': _L1_gnn_in['rel_att_b2'], 'L1_gnn_node_fc_W': _L1_gnn_in['node_fc_W'], 'L1_gnn_node_fc_b': _L1_gnn_in['node_fc_b'], 'L1_gnn_edge_fc_W': _L1_gnn_in['edge_fc_W'], 'L1_gnn_edge_fc_b': _L1_gnn_in['edge_fc_b'], 'L1_gnn_out_fc_W': _L1_gnn_in['out_fc_W'], 'L1_gnn_out_fc_b': _L1_gnn_in['out_fc_b'], 'L1_gnn_gate_W': _L1_gnn_in['gate_W'], 'L1_gnn_gate_b': _L1_gnn_in['gate_b']}

def reference(x, src, dst, edge_attr_64, edge_weight, L0_gnn_Wm, L0_gnn_bm, L0_gnn_W1, L0_gnn_b1, L0_gnn_W2, L0_gnn_b2, L1_gnn_node_att_W, L1_gnn_rel_att_W, L1_gnn_rel_att_W1, L1_gnn_rel_att_b1, L1_gnn_rel_att_W2, L1_gnn_rel_att_b2, L1_gnn_node_fc_W, L1_gnn_node_fc_b, L1_gnn_edge_fc_W, L1_gnn_edge_fc_b, L1_gnn_out_fc_W, L1_gnn_out_fc_b, L1_gnn_gate_W, L1_gnn_gate_b):
    import jax
    import jax.numpy as jnp

    def _L0_gnn_ref(z, edge_weight, edge_src, edge_dst, Wm, bm, W1, b1, W2, b2):
        import jax, jax.numpy as jnp
        import numpy as np
        N_NODES = 6250
        N_EDGES = 100000
        HID = 128
        n, H = z.shape
        Wd, Ws, ww = (Wm[:H], Wm[H:2 * H], Wm[2 * H])
        msgs = z[edge_dst] @ Wd + z[edge_src] @ Ws + edge_weight[:, None] * ww[None, :] + bm
        agg = jax.ops.segment_max(msgs, edge_dst, num_segments=n)
        deg = jax.ops.segment_sum(jnp.ones_like(edge_weight), edge_dst, num_segments=n)
        agg = jnp.where(deg[:, None] > 0, agg, jnp.zeros((), dtype=z.dtype))
        W1a, W1b = (W1[:H], W1[H:])
        hidden = jax.nn.relu(z @ W1a + agg @ W1b + b1)
        return hidden @ W2 + b2

    def _L1_gnn_ref(node_features, edge_features, src, dst, node_att_W, rel_att_W, rel_att_W1, rel_att_b1, rel_att_W2, rel_att_b2, node_fc_W, node_fc_b, edge_fc_W, edge_fc_b, out_fc_W, out_fc_b, gate_W, gate_b):
        import jax, jax.numpy as jnp
        import numpy as np
        N, E, D, DE, M, K = (2500, 40000, 128, 64, 3, 3)

        def _seg_softmax(x, seg, n):
            m = jax.ops.segment_max(x, seg, num_segments=n)
            e = jnp.exp(x - m[seg])
            z = jax.ops.segment_sum(e, seg, num_segments=n)
            return e / z[seg]
        n = node_features.shape[0]
        kk = node_att_W.shape[0]
        mm = rel_att_W.shape[0]
        h = node_features @ node_fc_W + node_fc_b
        he = edge_features @ edge_fc_W + edge_fc_b
        hs, hd = (h[src], h[dst])
        a = jnp.sum(hs * hd, axis=-1)
        t = jax.nn.relu(jnp.einsum('ed,mdf->emf', he, rel_att_W1) + rel_att_b1[None])
        g = jax.nn.sigmoid(jnp.einsum('emf,mf->em', t, rel_att_W2) + rel_att_b2[None])
        alpha = _seg_softmax(a, dst, n)
        beta = _seg_softmax(g, dst, n)
        s_att = jnp.einsum('ed,kdf->ef', hs, node_att_W)
        h_att = jax.ops.segment_sum(alpha[:, None] * s_att, dst, num_segments=n) / kk
        t_rel = jnp.einsum('ed,mdf->emf', hs, rel_att_W)
        msg_rel = jnp.einsum('em,emf->ef', beta, t_rel)
        h_rel = jax.ops.segment_sum(msg_rel, dst, num_segments=n) / mm
        h_red = jax.nn.relu(jnp.concatenate([h_att, h_rel], axis=-1) @ out_fc_W + out_fc_b)
        deg = jax.ops.segment_sum(jnp.ones((src.shape[0],), h.dtype), dst, num_segments=n)
        h_out = jnp.where(deg[:, None] > 0, h_red, h)
        gate = jax.nn.sigmoid(node_features @ gate_W + gate_b)
        return gate * h_out + (1.0 - gate) * node_features
    x = _layernorm(x + _L0_gnn_ref(x, edge_weight, src, dst, L0_gnn_Wm, L0_gnn_bm, L0_gnn_W1, L0_gnn_b1, L0_gnn_W2, L0_gnn_b2), axis=-1)
    x = _layernorm(x + _L1_gnn_ref(x, edge_attr_64, src, dst, L1_gnn_node_att_W, L1_gnn_rel_att_W, L1_gnn_rel_att_W1, L1_gnn_rel_att_b1, L1_gnn_rel_att_W2, L1_gnn_rel_att_b2, L1_gnn_node_fc_W, L1_gnn_node_fc_b, L1_gnn_edge_fc_W, L1_gnn_edge_fc_b, L1_gnn_out_fc_W, L1_gnn_out_fc_b, L1_gnn_gate_W, L1_gnn_gate_b), axis=-1)
    return x

_drawn_inputs = setup_inputs


def setup_inputs(seed=0):
    import zlib

    import numpy as np

    out = dict(_drawn_inputs(seed))
    spreads = {'L1_gnn_node_fc_b': (0.0, 0.8),
     'L1_gnn_edge_fc_b': (0.0, 2.0),
     'L1_gnn_out_fc_b': (0.0, 0.408)}
    factors = {'edge_attr_64': 105.953,
     'edge_weight': 8.0,
     'L1_gnn_rel_att_W': 4.132,
     'L1_gnn_rel_att_W1': 105.371,
     'L1_gnn_rel_att_b1': 200.0,
     'L1_gnn_rel_att_W2': 112.187,
     'L1_gnn_rel_att_b2': 200.0,
     'L1_gnn_edge_fc_W': 109.829,
     'L1_gnn_gate_W': 4.436}
    for name, (base, spread) in spreads.items():
        noise = np.random.default_rng([zlib.crc32(name.encode()), seed]).standard_normal(out[name].shape)
        drawn = base * np.exp(spread * noise) if base else spread * noise
        out[name] = jnp.asarray(drawn.astype(out[name].dtype))
    for name, factor in factors.items():
        out[name] = (out[name] * factor).astype(out[name].dtype)
    return out
```

```python
from contextlib import ExitStack

import concourse.bass as bass
from concourse import mybir

F32 = mybir.dt.float32
I32 = mybir.dt.int32
BF16 = mybir.dt.bfloat16
F32R = mybir.dt.float32r
ALU = mybir.AluOpType
ACT = mybir.ActivationFunctionType
X = mybir.AxisListType.X

P = 128
N, E, D, DE, M = 6250, 100000, 128, 64, 3
NT = -(-E // P)
TC = -(-NT // P)
W = 32
JC = 8
JP = JC * P
GJ = 4
NG = 4
IJ = GJ * NG
NBLK = -(-N // P)
CB = 7
CN = CB * P
NCH = NBLK // CB
NP = NBLK * P
ACCW = NP + W
BIG = float(2.0 ** 100)
PAD_DST = 8191
SRC, DST, WGT, ST, EN, FIRST, START = 0, P, 2 * P, 3 * P, 4 * P, 5 * P, 5 * P + 1
TW = 5 * P + 8
FLAT = JP * P // P
EPS = 1e-5
MAXIT = -(-(NT + -(-N // W)) // IJ)
assert MAXIT * IJ + IJ <= JP and NBLK == CB * NCH and NT < PAD_DST


class Count:

    def __init__(self, eng, sem, base=0):
        self.eng, self.sem, self.base, self.n = eng, sem, base, 0

    def add(self, ins):
        self.n += 1
        ins.then_inc(self.sem, 1)
        return self.n

    def wait(self, n=None):
        self.eng.wait_ge(self.sem, self.base + (self.n if n is None else n))

    def link(self, ins):
        self.add(ins)
        self.wait()


def split3(c, x, rest, parts):
    v = c.eng
    c.link(v.tensor_copy(parts[0], x))
    c.link(v.tensor_tensor(rest, x, parts[0], ALU.subtract))
    c.link(v.tensor_copy(parts[1], rest))
    c.link(v.tensor_tensor(rest, rest, parts[1], ALU.subtract))
    c.link(v.tensor_copy(parts[2], rest))


def sems(nc, ctx, *names):
    return [ctx.enter_context(nc.semaphore(n)) for n in names]


def tensors(nc, ctx):
    def sb(name, shape, dt=F32):
        return ctx.enter_context(nc.sbuf_tensor(name, shape, dt))

    t = {}
    t["ident"] = sb("ident", [P, P])
    t["ones"] = sb("ones", [P, P])
    t["iota_w"] = sb("iota_w", [P, GJ, W])
    t["base_row"] = sb("base_row", [1, JP + IJ], I32)
    t["nit"] = sb("nit", [P, 1], I32)
    t["src_col"] = sb("src_col", [P, JP + IJ], I32)
    t["rel_col"] = sb("rel_col", [P, JP])
    t["end_col"] = sb("end_col", [P, JP])
    t["tile_of_job"] = sb("tile_of_job", [P, JC], I32)
    t["hT"] = sb("hT", [P, ACCW])
    t["has_n"] = sb("has_n", [P, NBLK])
    t["gate_n"] = sb("gate_n", [P, NBLK])
    t["acc"] = sb("acc", [P, 4, ACCW])
    t["gate_col"] = sb("gate_col", [P, M, JP])
    t["att_col"] = sb("att_col", [P, JP])
    t["psum"] = [ctx.enter_context(nc.psum_tensor(f"bank{i}", [P, 512], F32)) for i in range(8)]
    return t


def region(nc, ctx, name, words):
    return Carve(ctx.enter_context(nc.sbuf_tensor(name, [P, words], F32))[:, :])


class Carve:

    def __init__(self, region):
        self.region, self.at = region, 0

    def __call__(self, cols, dt=F32, parts=P):
        words = cols if dt in (F32, I32) else -(-cols // 2)
        ap = self.region[0:parts, self.at:self.at + words]
        self.at += words
        assert self.at <= self.region.shape[1], self.at
        return ap if dt == F32 else ap.bitcast(dt)


def phase_tables(nc, t, i, d):
    with ExitStack() as ctx:
        (ld, ldw, cst, ch, stt, peS, peR, jr, peT, cpT, flat, back, pb, bcp, brow) = sems(
            nc, ctx, "a_loaded", "a_ws_loaded", "a_consts", "a_chain", "a_tiles_stored",
            "a_prefix_done", "a_rows_done", "a_jobs_gathered", "a_transposed", "a_transposed_copied",
            "a_flat_stored", "a_base_stored", "a_b_product", "a_b_copied", "a_base_row")
        ldx = sems(nc, ctx, "a_x_even_loaded", "a_x_odd_loaded")
        bst = sems(nc, ctx, "a_b_even_stored", "a_b_odd_stored")
        ca = region(nc, ctx, "a_region", 12600)
        v3 = lambda ap, a: ap.rearrange("p (a b) -> p a b", a=a)
        dI = v3(ca(TC * P, I32), TC)
        prevI = v3(ca(TC * P, I32), TC)
        nextI = v3(ca(TC * P, I32), TC)
        srcI = v3(ca(TC * P, I32), TC)
        accf = t["acc"][:, :, :].rearrange("p a b -> p (a b)")
        cb = Carve(accf)
        rec = v3(cb(TC * TW), TC)
        job = v3(cb(JC * TW), JC)
        rel = v3(cb(JP), JC)
        valid = v3(cb(JP), JC)
        relend = v3(cb(JP), JC)
        keep = v3(cb(JP), JC)
        stop = v3(cb(JP), JC)
        rst = v3(cb(JP, BF16), JC)
        wpart = [v3(ca(JP, BF16), JC) for _ in range(3)]
        wrest = v3(cb(JP), JC)
        ww, wwrest = ca(P, parts=1), ca(P, parts=1)
        wwpart = [ca(P, BF16, parts=1) for _ in range(3)]
        zero = ca(M * P)
        srow = cb(TC * P)
        cmp = cb(TC * P)
        upper = ca(P)
        tnum = ca(TC)
        jnum = ca(JC)
        km, kcum, kall = ca(TC), ca(TC), ca(1)
        kmI = ca(TC, I32)
        tj = ca(JC)
        base = ca(JC)
        tmp8 = ca(JC)
        baseI = ca(P, I32, parts=JC)
        ws = ca(P)
        xr = [ca(CN), ca(CN)]
        bo = [ca(CN), ca(CN)]
        bank = t["psum"]
        ident, ones = t["ident"], t["ones"]
        block = ctx.enter_context(nc.Block())
        NTR = 5

        @block.gpsimd
        def _(pool):
            c = Count(pool, cst)
            c.add(nc.gpsimd.memset(ident[:, :], 0.0))
            c.add(nc.gpsimd.memset(ones[:, :], 1.0))
            c.wait()
            c.add(nc.gpsimd.affine_select(out=ident[:, :], in_=ident[:, :], compare_op=ALU.not_equal, fill=1.0,
                                          base=0, pattern=[[-1, P]], channel_multiplier=1))
            c.add(nc.gpsimd.affine_select(out=upper, in_=ones[:, :], compare_op=ALU.is_gt, fill=0.0,
                                          base=0, pattern=[[1, P]], channel_multiplier=-1))
            c.add(nc.gpsimd.iota(tnum, [[P, TC]], base=0, channel_multiplier=1, allow_small_or_imprecise_dtypes=True))
            c.add(nc.gpsimd.iota(jnum, [[P, JC]], base=0, channel_multiplier=1, allow_small_or_imprecise_dtypes=True))
            c.add(nc.gpsimd.iota(t["iota_w"][:, :, :], [[0, GJ], [1, W]], base=0, channel_multiplier=0,
                                 allow_small_or_imprecise_dtypes=True))
            c.add(nc.gpsimd.memset(t["src_col"][:, JP:], 0))
            c.add(nc.gpsimd.memset(t["base_row"][:, JP:], 0))
            assert c.n == 9
            pool.wait_ge(stt, 16)
            pool.wait_ge(ch, CH_TJ)
            for k in range(JC):
                pool.indirect_dma_start(job[:, k, :], None, d["tiles"],
                                        bass.IndirectOffsetOnAxis(t["tile_of_job"][:, k:k + 1], 0)).then_inc(jr, 16)

        @block.sync
        def _(sp):
            def tiles(ap, off):
                return ap[off:off + TC * P * P].rearrange("(c p e) -> p c e", p=P, e=P)
            sp.dma_start(dI, tiles(i["dst"], 1)).then_inc(ld, 16)
            sp.dma_start(prevI, tiles(i["dst"], 0)).then_inc(ld, 16)
            sp.dma_start(nextI, tiles(i["dst"], 2)).then_inc(ld, 16)
            sp.dma_start(srcI, tiles(i["src"], 0)).then_inc(ld, 16)
            sp.dma_start(rec[:, :, WGT:WGT + P], tiles(i["w"], 0)).then_inc(ld, 16)
            sp.dma_start(ws, i["Wm"][D:2 * D, :]).then_inc(ldw, 16)
            for c in range(2):
                sp.dma_start(xr[c], i["xT"][:, c * CN:(c + 1) * CN]).then_inc(ldx[c % 2], 16)
            sp.dma_start(ww, i["Wm"][2 * D:2 * D + 1, :]).then_inc(ldw, 16)
            sp.wait_ge(ch, CH_REC)
            sp.dma_start(d["tiles"].rearrange("(c p) w -> p c w", p=P), rec).then_inc(stt, 16)
            sp.dma_start(d["gates"][NT // IJ * IJ:TC * P, :], zero[0:TC * P - NT // IJ * IJ, :]).then_inc(flat, 16)
            for a in range(3):
                for b in range(3):
                    sp.dma_start(d["ww9"][3 * a + b:3 * a + b + 1, :], wwpart[a]).then_inc(flat, 16)
            for c in range(NCH):
                sp.wait_ge(bcp, c + 1)
                sp.dma_start(d["B"][c * CN:(c + 1) * CN, :].rearrange("(b p) f -> p b f", p=P),
                             v3(bo[c % 2], CB)).then_inc(bst[c % 2], 16)
                if c + 2 < NCH:
                    sp.wait_ge(pb, c + 1)
                    sp.dma_start(xr[c % 2], i["xT"][:, (c + 2) * CN:(c + 3) * CN]).then_inc(ldx[c % 2], 16)
            sp.wait_ge(ch, CH_FLAGS)
            jrow = lambda ap: ap.rearrange("(c p e) -> p c e", p=P, e=P)
            sp.dma_start(jrow(d["valid"]), valid).then_inc(flat, 16)
            sp.dma_start(jrow(d["keep"]), keep).then_inc(flat, 16)
            sp.dma_start(jrow(d["stop"]), stop).then_inc(flat, 16)
            sp.dma_start(jrow(d["reset"]), rst).then_inc(flat, 16)
            for a in range(3):
                for b in range(3):
                    sp.dma_start(jrow(d["w9"][3 * a + b, :]), wpart[b]).then_inc(flat, 16)
            sp.wait_ge(ch, CH_BASE)
            sp.dma_start(d["base"].rearrange("(c p) -> c p", p=P), baseI).then_inc(back, 16)
            sp.wait_ge(back, 16)
            sp.dma_start(t["base_row"][0:1, 0:JP], d["base"].rearrange("(a n) -> a n", a=1)).then_inc(brow, 16)
            sp.wait_ge(flat, (4 + 9 + 9 + 1) * 16)
            sp.wait_ge(bst[0], 16 * (NCH - NCH // 2))
            sp.wait_ge(bst[1], 16 * (NCH // 2))
            sp.wait_ge(brow, 16)

        @block.vector
        def _(dve):
            c = Count(dve, ch)
            dve.wait_ge(ld, 5 * 16)
            c.add(nc.vector.tensor_copy(rec[:, :, DST:DST + P], dI))
            c.add(nc.vector.tensor_copy(rec[:, :, SRC:SRC + P], srcI))
            c.add(nc.vector.tensor_tensor(rec[:, :, ST:ST + P], dI, prevI, ALU.not_equal))
            c.add(nc.vector.tensor_tensor(rec[:, :, EN:EN + P], dI, nextI, ALU.not_equal))
            c.wait()
            dd = rec[:, :, DST:DST + P]
            real = v3(cmp, TC)
            c.link(nc.vector.scalar_tensor_tensor(real, dd, float(PAD_DST), dd, ALU.is_lt, ALU.mult))
            c.link(nc.vector.reduce_max(km, real, X))
            c.link(nc.vector.tensor_tensor(km, km, rec[:, :, DST], ALU.subtract))
            c.link(nc.vector.tensor_scalar(kmI, km, 0.0, None, ALU.max))
            c.link(nc.vector.tensor_single_scalar(kmI, kmI, 5, ALU.arith_shift_right))
            c.link(nc.vector.tensor_copy(km, kmI))
            c.add(nc.vector.memset(kcum[:, 0:1], 0.0))
            dve.wait_ge(cst, 9)
            c.add(nc.vector.tensor_tensor_scan(kcum[:, 1:TC], ones[:, 0:TC - 1], km[:, 0:TC - 1], 0.0,
                                               ALU.mult, ALU.add))
            c.link(nc.vector.reduce_sum(kall, km, X))
            assert c.n == CH_KM
            dve.wait_ge(peS, 1)
            c.add(nc.vector.tensor_tensor(rec[:, :, START], bank[0][:, 0:TC], tnum, ALU.add))
            c.link(nc.vector.tensor_copy(rec[:, :, FIRST], rec[:, :, DST]))
            c.add(nc.vector.tensor_copy(rec[:, :, START + 1:TW], rec[:, :, DST:DST + TW - START - 1]))
            c.add(nc.vector.memset(zero, 0.0))
            dve.wait_ge(ldw, 32)
            split3(c, ww, wwrest, wwpart)
            assert c.n == CH_REC
            c.link(nc.vector.tensor_scalar(t["nit"][:, :], bank[1][:, 0:1], float(NT + IJ - 1), None, ALU.add))
            c.link(nc.vector.tensor_single_scalar(t["nit"][:, :], t["nit"][:, :], 4, ALU.arith_shift_right))
            dve.wait_ge(peR, 1)
            c.add(nc.vector.tensor_copy(srow[:, 0:4 * P], bank[2][:, :]))
            c.link(nc.vector.tensor_copy(srow[:, 4 * P:TC * P], bank[3][:, 0:(TC - 4) * P]))
            for k in range(JC):
                c.link(nc.vector.tensor_scalar(cmp, srow, jnum[:, k:k + 1], 0.0, ALU.is_le, ALU.add,
                                               accum_out=tj[:, k:k + 1]))
            c.link(nc.vector.tensor_scalar(t["tile_of_job"][:, :], tj, -1.0, None, ALU.add))
            assert c.n == CH_TJ
            dve.wait_ge(jr, 16 * JC)
            c.link(nc.vector.tensor_tensor(tmp8, jnum, job[:, :, START], ALU.subtract))
            c.link(nc.vector.scalar_tensor_tensor(base, tmp8, float(W), job[:, :, FIRST], ALU.mult, ALU.add))
            c.link(nc.vector.tensor_scalar(base, base, float(N), None, ALU.min))
            c.link(nc.vector.tensor_tensor(rel, job[:, :, DST:DST + P],
                                           base.unsqueeze(2).to_broadcast([P, JC, P]), ALU.subtract))
            c.link(nc.vector.tensor_scalar(valid, rel, 0.0, None, ALU.is_ge))
            c.link(nc.vector.scalar_tensor_tensor(valid, rel, float(W), valid, ALU.is_lt, ALU.mult))
            c.add(nc.vector.tensor_tensor(stop, job[:, :, EN:EN + P], valid, ALU.mult))
            c.link(nc.vector.tensor_tensor(keep, job[:, :, ST:ST + P], valid, ALU.mult))
            c.add(nc.vector.tensor_scalar(keep, keep, -1.0, 1.0, ALU.mult, ALU.add))
            c.add(nc.vector.tensor_scalar(rst, job[:, :, ST:ST + P], -BIG, None, ALU.mult))
            c.link(nc.vector.scalar_tensor_tensor(relend, rel, 1.0, job[:, :, EN:EN + P], ALU.add, ALU.mult))
            c.link(nc.vector.tensor_scalar(relend, relend, -1.0, None, ALU.add))
            split3(c, job[:, :, WGT:WGT + P], wrest, wpart)
            assert c.n == CH_FLAGS
            dve.wait_ge(peT, 1)
            c.add(nc.vector.tensor_copy(baseI, bank[0][0:JC, 0:P]))
            assert c.n == CH_BASE
            for n, dst in enumerate((t["src_col"], t["rel_col"], t["end_col"])):
                for half in range(2):
                    dve.wait_ge(peT, 2 + 2 * n + half)
                    nc.vector.tensor_copy(dst[:, half * 512:half * 512 + 512],
                                          bank[2 + half][:, :]).then_inc(cpT, 1)

        @block.tensor
        def _(pe):
            pe.wait_ge(cst, 9)
            def product(c):
                pe.wait_ge(ldx[c % 2], 16 * (c // 2 + 1))
                if c:
                    pe.wait_ge(bcp, c)
                for b in range(CB):
                    o = bank[4 + b // 4][:, b % 4 * P:b % 4 * P + P]
                    last = nc.tensor.matmul(o, xr[c % 2][:, b * P:(b + 1) * P], ws, start=True, stop=True)
                last.then_inc(pb, 1)
            pe.wait_ge(ldw, 32)
            product(0)
            pe.wait_ge(ch, CH_KM)
            nc.tensor.matmul(bank[0][:, 0:TC], upper, km, start=True, stop=False)
            nc.tensor.matmul(bank[0][:, 0:TC], ones[:, :], kcum, start=False, stop=True)
            nc.tensor.matmul(bank[1][:, 0:1], ones[:, :], kall, start=True, stop=True).then_inc(peS, 1)
            pe.wait_ge(ch, CH_KM + 2)
            for k in range(TC):
                last = nc.tensor.matmul(bank[2 + k // 4][:, k % 4 * P:k % 4 * P + P],
                                        rec[:, k, START:START + 1].to_broadcast([P, P]), ident[:, :],
                                        start=True, stop=True)
            last.then_inc(peR, 1)
            for c in range(1, NCH):
                product(c)
            pe.wait_ge(ch, CH_FLAGS)
            nc.tensor.matmul(bank[0][0:JC, 0:P], base, ident[:, :], start=True, stop=True).then_inc(peT, 1)
            for n, field in enumerate((job[:, :, SRC:SRC + P], rel, relend)):
                for half in range(2):
                    if n:
                        pe.wait_ge(cpT, 2 * n - 1 + half)
                    for k in range(4):
                        last = nc.tensor.matmul(bank[2 + half][:, k * P:(k + 1) * P], field[:, half * 4 + k, :],
                                                ident[:, :], start=True, stop=True)
                    last.then_inc(peT, 1)

        @block.scalar
        def _(act):
            for c in range(NCH):
                act.wait_ge(pb, c + 1)
                if c >= 2:
                    act.wait_ge(bst[c % 2], 16 * (c // 2))
                nc.scalar.activation(bo[c % 2][:, 0:4 * P], bank[4][:, :], ACT.Copy)
                nc.scalar.activation(bo[c % 2][:, 4 * P:CN], bank[5][:, 0:CN - 4 * P], ACT.Copy).then_inc(bcp, 1)


CH_KM = 13
CH_REC = CH_KM + 3 + 1 + 5
CH_TJ = CH_REC + 2 + 2 + JC + 1
CH_FLAGS = CH_TJ + 12 + 5
CH_BASE = CH_FLAGS + 1


def group_bases(nc, t, eng_type, it, q):
    _, v = nc.values_load_multi_w_load_instructions(
        t["base_row"][0:1, bass.ds(it * IJ + q * GJ, GJ)], engines=[eng_type], min_val=0, max_val=N,
        skip_runtime_bounds_check_because="the table's entries are held to at most N when it is made")
    return v


def iterations(eng, t):
    return eng.value_load(t["nit"][0:1, 0:1], min_val=NT // IJ, max_val=MAXIT)


def gather_rows(nc, pool, t, table, idx, rows, idx_ready, slot_free, gathered, stored=None, ahead=False):
    nit = iterations(pool, t)

    def group(it, q):
        pool.wait_ge(idx_ready, it * NG + (q + 1))
        for sem, per in slot_free:
            pool.wait_ge(sem, it * (NG * per) + (q + 1) * per)
        if stored:
            pool.wait_ge(stored[q], it * 16 + 16)
        hold(pool)
        for j in range(GJ):
            s = q * GJ + j
            pool.indirect_dma_start(rows[:, s, :], None, table,
                                    bass.IndirectOffsetOnAxis(idx[:, s:s + 1], 0)).then_inc(gathered[q], 16)

    with pool.Fori(0, nit) as it:
        for q in range(NG):
            group(it, q)
    if ahead:
        group(nit, 0)


def phase_layer0(nc, t, i, d):
    with ExitStack() as ctx:
        (wld, pre, pre2, zero, idxr, p1, scd, t2, ehd, st, ex, acd, es, tm, ra, rd, dt, gc, hp, ch) = sems(
            nc, ctx, "b_weights_loaded", "b_fold_product", "b_fold_copied", "b_zeroed", "b_idx_ready",
            "b_transposed_in", "b_scanned", "b_transposed_back", "b_ends_built", "b_back_copied",
            "b_ends_picked", "b_windows_written", "b_features_split", "b_mlp_product", "b_relu_act",
            "b_relu_dve", "b_dots_done", "b_gates_copied", "b_high_parts", "b_chain")
        gat = sems(nc, ctx, *[f"b_gathered{q}" for q in range(NG)])
        rl = sems(nc, ctx, *[f"b_resets_loaded{q}" for q in range(NG)])
        wl = sems(nc, ctx, *[f"b_weights_row_loaded{q}" for q in range(NG)])
        el = sems(nc, ctx, *[f"b_edge_features_loaded{q}" for q in range(NG)])
        gst = sems(nc, ctx, *[f"b_gates_stored{q}" for q in range(2)])
        wfr = ctx.enter_context(nc.sbuf_tensor("b_wf", [P, 2 * M * P], F32R))
        ear = [ctx.enter_context(nc.sbuf_tensor(f"b_ea{q}", [P, GJ * P], F32R)) for q in range(2)]
        ca = region(nc, ctx, "b_region", 10800)
        cb = Carve(t["acc"][:, 2:4, :].rearrange("p a b -> p (a b)"))
        G4 = GJ * P
        rows = ca(IJ * P).rearrange("p (s f) -> p s f", f=P)
        idx = ca(IJ, I32)
        rst = [ca(G4, BF16) for _ in range(NG)]
        w9 = [cb(G4, BF16) for _ in range(NG)]
        scan = [ca(G4) for _ in range(2)]
        back = [ca(G4) for _ in range(2)]
        ends = [ca(GJ * W) for _ in range(NG)]
        ends16 = [ca(GJ * W, BF16) for _ in range(NG)]
        ea = [cb(G4) for _ in range(NG)]
        rt = [[ca(G4) for _ in range(M)] for _ in range(2)]
        gout = [cb(G4) for _ in range(2)]
        bf, b1, w2 = ca(M), ca(M), ca(M)
        w2m = ca(M * W)
        ww9 = cb(P, BF16)
        ones16 = cb(P, BF16)
        weT, w1, be = cb(2 * DE, parts=DE), cb(M * P, parts=DE), cb(1, parts=DE)
        start = cb(16)
        bank = t["psum"]
        p1b, p2b, p3b, tb, gb = bank[0:2], bank[2], bank[3], bank[4:7], bank[7]
        ident, ones = t["ident"], t["ones"]
        P3 = [p3b[:, h * 256:h * 256 + 256].rearrange("p (a j w) -> p a j w", a=2, j=GJ) for h in range(2)]
        block = ctx.enter_context(nc.Block())
        CREDIT = NG

        @block.gpsimd
        def _(pool):
            for n, (s, per) in enumerate([(scd, 1), (p1, 1), (t2, 1), (ex, 1), (st, 1), (acd, GJ), (rd, 1), (dt, 1),
                                          (ra, 2), (tm, M), (gc, 1), (es, 1), (gst[0], 4), (gst[1], 4)]):
                nc.gpsimd.memset(start[:, n:n + 1], 0.0).then_inc(s, per * CREDIT)
            gather_rows(nc, pool, t, d["B"], idx, rows, idxr, [(p1, 1)], gat, ahead=True)

        @block.sync
        def _(sp):
            sp.dma_start(weT[:, 0:DE], i["weT"]).then_inc(wld, 16)
            sp.dma_start(weT[:, DE:2 * DE], i["weT"]).then_inc(wld, 16)
            sp.dma_start(w1.rearrange("d (m f) -> d m f", m=M), i["w1"].rearrange("m d f -> d m f")).then_inc(wld, 16)
            sp.dma_start(be, i["be"]).then_inc(wld, 16)
            sp.dma_start(b1, i["b1T"]).then_inc(wld, 16)
            sp.dma_start(w2, i["w2T"]).then_inc(wld, 16)
            sp.wait_ge(zero, 2)
            sp.dma_start(ww9[0:9, :], d["ww9"]).then_inc(wld, 16)
            nit = iterations(sp, t)

            def load(it, q):
                s = q % NG
                at = (it * NG + q) * G4
                sp.wait_ge(scd, it * NG + (q + 1))
                hold(sp)
                sp.dma_start(rst[s], d["reset"][bass.ds(at, G4)].partition_broadcast(P)).then_inc(rl[s], 16)
                sp.wait_ge(p1, it * NG + (q + 1))
                hold(sp)
                sp.dma_start(w9[s][0:9, :], d["w9"][:, bass.ds(at, G4)]).then_inc(wl[s], 16)
                sp.wait_ge(es, it * NG + (q + 1))
                hold(sp)
                for half in range(2):
                    sp.dma_start(ea[s][half * DE:(half + 1) * DE, :],
                                 i["eaT"][bass.ds(it * NG + q, 1), :, :].rearrange("a d e -> (a d) e")
                                 ).then_inc(el[s], 16)

            load(0, 0)
            load(0, 1)
            with sp.Fori(0, nit) as it:
                for q in range(NG):
                    load(it, q + 2)
                    sp.wait_ge(gc, it * NG + (q + 1 + CREDIT))
                    hold(sp)
                    store_gates(sp, d, gout[q % 2], it * NG + q, gst[q % 2])
            sp.wait_ge(wld, 7 * 16)
            sp.wait_ge(rl[1], nit * 16 + 16)
            sp.wait_ge(wl[1], nit * 16 + 16)
            hold(sp)
            sp.wait_ge(el[1], nit * 32 + 32)
            hold(sp)
            for n in range(2):
                sp.wait_ge(gst[n], nit * 32 + 16)
            hold(sp)

        @block.tensor
        def _(pe):
            pe.wait_ge(wld, 7 * 16)
            nc.tensor.matmul(bank[0][:, 0:M * P], weT, w1, start=True, stop=True)
            for m in range(M):
                last = nc.tensor.matmul(bank[1][:, m:m + 1], w1[:, m * P:(m + 1) * P], be, start=True, stop=True)
            last.then_inc(pre, 1)
            pe.wait_ge(pre2, 1)
            nit = iterations(pe, t)

            def rows_in(it, q):
                s = q % NG
                pe.wait_ge(gat[s], it * 64 + 64 * (q // NG + 1))
                pe.wait_ge(wl[s], it * 16 + 16 * (q // NG + 1))
                pe.wait_ge(scd, it * NG + (q - 2 + 1 + CREDIT))
                b = p1b[q % 2]
                nc.tensor.matmul(b[:, :], ww9, w9[s], start=True, stop=False)
                for j in range(GJ):
                    last = nc.tensor.matmul(b[:, j * P:(j + 1) * P], rows[:, s * GJ + j, :], ident[:, :],
                                            start=False, stop=(j == GJ - 1))
                last.then_inc(p1, 1)

            def mlp(it, q):
                pe.wait_ge(es, it * NG + (q + 1 + CREDIT))
                for m in range(M):
                    if m < 2:
                        pe.wait_ge(ra, it * (2 * NG) + (2 * (q - 1 + CREDIT) + m + 1))
                    else:
                        pe.wait_ge(rd, it * NG + (q + CREDIT))
                    nc.tensor.matmul(tb[m][:, :], wfr[:, m * P:(m + 1) * P], ear[q % 2][:, :], start=True, stop=False)
                    nc.tensor.matmul(tb[m][:, :], wfr[:, (M + m) * P:(M + m + 1) * P], ear[q % 2][:, :],
                                     start=False, stop=True).then_inc(tm, 1)

            def rows_back(it, q):
                pe.wait_ge(scd, it * NG + (q + 1 + CREDIT))
                pe.wait_ge(st, it * NG + (q + CREDIT))
                for j in range(GJ):
                    last = nc.tensor.transpose(p2b[:, j * P:(j + 1) * P], scan[q % 2][:, j * P:(j + 1) * P],
                                               ident[:, :])
                last.then_inc(t2, 1)

            def dots(it, q):
                pe.wait_ge(ra, it * (2 * NG) + 2 * (q + 1 + CREDIT))
                pe.wait_ge(rd, it * NG + (q + 1 + CREDIT))
                pe.wait_ge(gc, it * NG + (q + CREDIT))
                for m in range(M):
                    last = nc.tensor.matmul(gb[m * W:(m + 1) * W, :], w2m[:, m * W:(m + 1) * W], rt[q % 2][m],
                                            start=True, stop=True)
                last.then_inc(dt, 1)

            def pick(it, q):
                pe.wait_ge(st, it * NG + (q + 1 + CREDIT))
                pe.wait_ge(ehd, it * (2 * NG) + 2 * (q + 1))
                pe.wait_ge(acd, it * (NG * GJ) + (q - 2 + 1 + CREDIT) * GJ)
                for j in range(GJ):
                    nc.tensor.matmul(P3[q % 2][:, 0, j, :], back[q % 2][:, j * P:(j + 1) * P],
                                     ends[q][:, j * W:(j + 1) * W], start=True, stop=True)
                nc.tensor.matmul(P3[q % 2][:, 1, :, :].rearrange("p j w -> p (j w)"), ones16, ends16[q],
                                 start=True, stop=True).then_inc(ex, 1)

            rows_in(0, 0)
            mlp(0, 0)
            rows_back(0, 0)
            with pe.Fori(0, nit) as it:
                for q in range(NG):
                    rows_in(it, q + 1)
                    mlp(it, q + 1)
                    dots(it, q)
                    pick(it, q)
                    rows_back(it, q + 1)

        @block.scalar
        def _(act):
            nit = iterations(act, t)
            act.wait_ge(zero, 2)

            def relus(it, q):
                for m in range(2):
                    act.wait_ge(tm, it * (3 * NG) + (3 * (q + CREDIT) + m + 1))
                    if m == 0:
                        act.wait_ge(dt, it * NG + (q - 2 + 1 + CREDIT))
                    nc.scalar.activation(rt[q % 2][m], tb[m][:, :], ACT.Relu, bias=bf[:, m:m + 1]).then_inc(ra, 1)

            def copy_back(it, q):
                act.wait_ge(t2, it * NG + (q + 1 + CREDIT))
                act.wait_ge(ex, it * NG + (q - 2 + 1 + CREDIT))
                nc.scalar.activation(back[q % 2], p2b[:, :], ACT.Copy).then_inc(st, 1)

            relus(0, 0)
            copy_back(0, 0)
            with act.Fori(0, nit) as it:
                for q in range(NG):
                    base = group_bases(nc, t, mybir.EngineType.Activation, it, q)
                    relus(it, q + 1)
                    act.wait_ge(ex, it * NG + (q + 1 + CREDIT))
                    for j in range(GJ):
                        act.wait_ge(acd, it * (NG * GJ) + ((q + CREDIT) * GJ + j))
                        nc.scalar.activation(t["acc"][:, 0:2, bass.ds(base[j], W)], P3[q % 2][:, :, j, :],
                                             ACT.Copy).then_inc(acd, 1)
                    copy_back(it, q + 1)

        @block.vector
        def _(dve):
            c = Count(dve, ch)
            c.add(nc.vector.memset(scan[(NG - 1) % 2], -BIG))
            nc.vector.memset(t["acc"][:, 0:2, :], 0.0).then_inc(zero, 1)
            c.add(nc.vector.memset(ww9, 0.0))
            c.add(nc.vector.memset(ones16, 1.0))
            c.add(nc.vector.memset(w2m, 0.0))
            for q in range(NG - 1):
                c.add(nc.vector.memset(w9[q], 0.0))
            c.wait()
            nc.vector.memset(w9[NG - 1], 0.0).then_inc(zero, 1)
            nc.vector.tensor_copy(idx, t["src_col"][:, 0:IJ]).then_inc(idxr, NG)
            dve.wait_ge(pre, 1)
            c.link(nc.vector.tensor_copy(wfr[:, 0:M * P], bank[0][:, 0:M * P]))
            c.add(nc.vector.tensor_copy(w2m.rearrange("p (m w) -> p m w", m=M)[:, :, 0], w2))
            c.link(nc.vector.tensor_tensor(wfr[:, M * P:2 * M * P], bank[0][:, 0:M * P],
                                           wfr[:, 0:M * P].bitcast(F32), ALU.subtract))
            nc.vector.tensor_tensor(bf, bank[1][:, 0:M], b1, ALU.add).then_inc(pre2, 1)
            c.wait()
            nit = iterations(dve, t)
            iota = t["iota_w"][:, :, :]

            def ahead(it, q):
                s = q % NG
                g = it * NG
                again = q // NG
                col = it * IJ + q * GJ
                dve.wait_ge(el[s], it * 32 + 32 * (again + 1))
                dve.wait_ge(tm, it * (3 * NG) + 3 * (q - 2 + 1 + CREDIT))
                nc.vector.tensor_copy(ear[q % 2][:, :], ea[s]).then_inc(hp, 1)
                dve.wait_ge(hp, g + (q + 1))
                nc.vector.tensor_tensor(ear[q % 2][DE:P, :], ea[s][DE:P, :], ear[q % 2][DE:P, :].bitcast(F32),
                                        ALU.subtract).then_inc(es, 1)
                dve.wait_ge(rl[s], it * 16 + 16 * (again + 1))
                dve.wait_ge(p1, g + (q + 1 + CREDIT))
                dve.wait_ge(t2, g + (q - 2 + 1 + CREDIT))
                dve.wait_ge(scd, g + (q + CREDIT))
                nc.vector.tensor_tensor_scan(scan[q % 2], rst[s], p1b[q % 2][:, :],
                                             scan[(q + 1) % 2][:, G4 - 1:G4], ALU.add, ALU.max).then_inc(scd, 1)
                dve.wait_ge(ex, g + (q + 1))
                rel = t["end_col"][:, bass.ds(col, GJ)].unsqueeze(2).to_broadcast([P, GJ, W])
                nc.vector.tensor_tensor(ends[s].rearrange("p (j w) -> p j w", j=GJ), iota, rel,
                                        ALU.is_equal).then_inc(ehd, 1)
                nc.vector.tensor_tensor(ends16[s].rearrange("p (j w) -> p j w", j=GJ), iota, rel,
                                        ALU.is_equal).then_inc(ehd, 1)
                dve.wait_ge(gat[s], it * 64 + 64 * (again + 1))
                hold(dve)
                nc.vector.tensor_copy(idx[:, s * GJ:(s + 1) * GJ],
                                      t["src_col"][:, bass.ds(col + IJ, GJ)]).then_inc(idxr, 1)
                dve.wait_ge(tm, it * (3 * NG) + 3 * (q + 1 + CREDIT))
                dve.wait_ge(dt, g + (q - 2 + 1 + CREDIT))
                nc.vector.tensor_scalar(rt[q % 2][2], tb[2][:, :], bf[:, 2:3], 0.0, ALU.add,
                                        ALU.max).then_inc(rd, 1)

            ahead(0, 0)
            with dve.Fori(0, nit) as it:
                for q in range(NG):
                    ahead(it, q + 1)
                    dve.wait_ge(dt, it * NG + (q + 1 + CREDIT))
                    dve.wait_ge(gst[q % 2], it * 32 + (16 * (q // 2) + 16))
                    nc.vector.tensor_copy(gout[q % 2][0:M * W, :], gb[0:M * W, :]).then_inc(gc, 1)


def hold(eng):
    eng.nop(nofuse=True)


def store_gates(sp, d, src, g, sem):
    sp.dma_start(d["gates"][bass.ds(g * GJ, GJ), :].rearrange("t (m e) -> m t e", m=M),
                 src[0:M * W:W, :].rearrange("m (t e) -> m t e", t=GJ)).then_inc(sem, 16)


def phase_softmax(nc, t, i, d, gates):
    heads = M if gates else 1
    with ExitStack() as ctx:
        (ld, gat, sg, tr, fs, cl, req, giv, xr, xd, ws, wl, tr2, tr2c, ch) = sems(
            nc, ctx, *[("c_" if gates else "e_") + n for n in (
                "loaded", "gathered", "sigmoid", "transposed", "flat_stored",
                "chunks_loaded", "carry_asked", "carry_given", "exp_asked", "exp_done", "weights_stored",
                "weights_loaded", "back_transposed", "back_copied", "chain")])
        ca = region(nc, ctx, "c_region" if gates else "e_region", 11400)
        valid, keep, stop = ca(FLAT), ca(FLAT), ca(FLAT)
        never, reset, go = ca(FLAT), ca(FLAT), ca(FLAT)
        v, f, b, e = ca(FLAT), ca(FLAT), ca(FLAT), ca(FLAT)
        mins = ca(3)
        minrow = [ca(P, parts=1) for _ in range(3)]
        row = ca(P, parts=1)
        crow = ca(P + 1, parts=1)
        ccol = ca(1)
        b2 = ca(M)
        if gates:
            cb = Carve(t["acc"][:, 2:4, :].rearrange("p a b -> p (a b)"))
            jg = cb(JC * M * P).rearrange("p (c m e) -> p c m e", c=JC, m=M)
            out = [cb(FLAT) for _ in range(M)]
            rows = [jg[:, :, m, :] for m in range(M)]
        else:
            rows = [v.rearrange("p (c e) -> p c e", e=P)]
            out = [v]
        bank = t["psum"]
        ident, ones = t["ident"], t["ones"]
        jrow = lambda ap: ap.rearrange("(c p e) -> p c e", p=P, e=P)
        chunk = lambda ap: ap.rearrange("(p n) -> p n", p=P)
        fwd, bwd = (f[:, FLAT - 1:FLAT], 0), (b[:, 0:1], 1)
        block = ctx.enter_context(nc.Block())

        @block.gpsimd
        def _(pool):
            if gates:
                for k in range(JC):
                    pool.indirect_dma_start(jg[:, k, :, :].rearrange("p m e -> p (m e)"), None,
                                            d["gates"][0:TC * P, :],
                                            bass.IndirectOffsetOnAxis(t["tile_of_job"][:, k:k + 1], 0)
                                            ).then_inc(gat, 16)

        @block.sync
        def _(sp):
            sp.dma_start(valid, chunk(d["valid"])).then_inc(ld, 16)
            sp.dma_start(keep, chunk(d["keep"])).then_inc(ld, 16)
            sp.dma_start(stop, chunk(d["stop"])).then_inc(ld, 16)
            if gates:
                sp.dma_start(b2, i["b2"].partition_broadcast(P)).then_inc(ld, 16)
            for m in range(heads):
                sp.wait_ge(sg, m + 1)
                sp.dma_start(jrow(d["flat"][m, :]), rows[m]).then_inc(fs, 16)
            sp.wait_ge(fs, 16 * heads)
            for m in range(heads):
                sp.wait_ge(ws, m * 17)
                sp.dma_start(v, chunk(d["flat"][m, :])).then_inc(cl, 16)
                sp.wait_ge(ws, m * 17 + 1)
                sp.dma_start(chunk(d["wflat"][m, :]), e).then_inc(ws, 16)
            sp.wait_ge(ws, 17 * heads)
            for m in range(heads):
                sp.dma_start(out[m].rearrange("p (c e) -> p c e", e=P), jrow(d["wflat"][m, :])).then_inc(wl, 16)

        @block.scalar
        def _(act):
            if gates:
                act.wait_ge(gat, 16 * JC)
                act.wait_ge(ld, 64)
                for m in range(M):
                    nc.scalar.activation(rows[m], rows[m], ACT.Sigmoid, bias=b2[:, m:m + 1]).then_inc(sg, 1)
            for m in range(heads):
                act.wait_ge(xr, m + 1)
                nc.scalar.activation(e, e, ACT.Exp).then_inc(xd, 1)

        @block.tensor
        def _(pe):
            if not gates:
                for k in range(JC):
                    last = nc.tensor.transpose(bank[2 + k // 4][:, k % 4 * P:k % 4 * P + P],
                                               t["att_col"][:, k * P:(k + 1) * P], ident[:, :])
                last.then_inc(tr, 1)
            n = 0
            for k in range(3):
                n += 1
                pe.wait_ge(req, n)
                nc.tensor.matmul(bank[0][0:1, 0:P], mins[:, k:k + 1], ident[:, :], start=True, stop=True
                                 ).then_inc(giv, 1)
            for m in range(heads):
                for last_state, off in (fwd, bwd, fwd, bwd):
                    n += 1
                    pe.wait_ge(req, n)
                    nc.tensor.matmul(bank[0][0:1, 0:P], last_state, ident[:, :], start=True, stop=True
                                     ).then_inc(giv, 1)
                    n += 1
                    pe.wait_ge(req, n)
                    nc.tensor.matmul(bank[1][:, 0:1], crow[:, off:off + P], ones[0:1, 0:1], start=True, stop=True
                                     ).then_inc(giv, 1)
            pe.wait_ge(wl, 16 * heads)
            for m in range(heads):
                for half in range(2):
                    if m:
                        pe.wait_ge(tr2c, 2 * m - 1 + half)
                    for k in range(4):
                        last = nc.tensor.transpose(bank[2 + half][:, k * P:(k + 1) * P],
                                                   out[m][:, (half * 4 + k) * P:(half * 4 + k + 1) * P], ident[:, :])
                    last.then_inc(tr2, 1)

        @block.vector
        def _(dve):
            c = Count(dve, ch)
            asked = [0]

            def ask(ins):
                asked[0] += 1
                ins.then_inc(req, 1)
                dve.wait_ge(giv, asked[0])

            if not gates:
                dve.wait_ge(tr, 1)
                c.add(nc.vector.tensor_copy(v[:, 0:512], bank[2][:, :]))
                nc.vector.tensor_copy(v[:, 512:FLAT], bank[3][:, :]).then_inc(sg, 1)
                c.wait()
            dve.wait_ge(ld, 64 if gates else 48)
            c.add(nc.vector.tensor_scalar(never, valid, 1.0, BIG, ALU.subtract, ALU.mult))
            c.add(nc.vector.tensor_scalar(reset, keep, 1.0, BIG, ALU.subtract, ALU.mult))
            c.link(nc.vector.tensor_scalar(go, stop, -1.0, 1.0, ALU.mult, ALU.add))
            for k, src in enumerate((reset, keep, go)):
                ask(nc.vector.tensor_reduce(mins[:, k:k + 1], src, X, ALU.min))
                c.link(nc.vector.tensor_copy(minrow[k], bank[0][0:1, 0:P]))

            def carried(last, through, op0, op1, init, back):
                c.wait()
                ask(nc.vector.memset(crow, init))
                c.link(nc.vector.tensor_copy(row, bank[0][0:1, 0:P]))
                if back:
                    ask(nc.vector.tensor_tensor_scan(crow[:, 0:P][:, ::-1], through[:, ::-1], row[:, ::-1], init,
                                                     op0, op1))
                else:
                    ask(nc.vector.tensor_tensor_scan(crow[:, 1:P + 1], through, row, init, op0, op1))
                c.link(nc.vector.tensor_copy(ccol, bank[1][:, 0:1]))

            def over(out_, keep_, x, minrow_, op0, op1, init):
                c.link(nc.vector.tensor_tensor_scan(out_, keep_, x, init, op0, op1))
                carried(out_, minrow_, op0, op1, init, False)
                c.link(nc.vector.tensor_tensor_scan(out_, keep_, x, ccol, op0, op1))

            def handed_back():
                c.link(nc.vector.tensor_tensor(f, f, stop, ALU.mult))
                c.link(nc.vector.tensor_tensor_scan(b[:, ::-1], go[:, ::-1], f[:, ::-1], 0.0, ALU.mult, ALU.add))
                carried(b, minrow[2], ALU.mult, ALU.add, 0.0, True)
                c.link(nc.vector.tensor_tensor_scan(b[:, ::-1], go[:, ::-1], f[:, ::-1], ccol, ALU.mult, ALU.add))

            for m in range(heads):
                dve.wait_ge(cl, 16 * (m + 1))
                c.link(nc.vector.tensor_tensor(v, v, valid, ALU.mult))
                c.link(nc.vector.tensor_tensor(v, v, never, ALU.add))
                over(f, reset, v, minrow[0], ALU.add, ALU.max, -BIG)
                handed_back()
                dve.wait_ge(ws, m * 17)
                nc.vector.tensor_tensor(e, v, b, ALU.subtract).then_inc(xr, 1)
                dve.wait_ge(xd, m + 1)
                c.link(nc.vector.tensor_tensor(e, e, valid, ALU.mult))
                over(f, keep, e, minrow[1], ALU.mult, ALU.add, 0.0)
                handed_back()
                c.link(nc.vector.tensor_scalar(b, b, 0.5, None, ALU.max))
                c.link(nc.vector.reciprocal(b, b))
                nc.vector.tensor_tensor(e, e, b, ALU.mult).then_inc(ws, 1)
            for m in range(heads):
                for half in range(2):
                    dve.wait_ge(tr2, 2 * m + half + 1)
                    dst = t["gate_col"][:, m, :] if gates else t["att_col"][:, :]
                    nc.vector.tensor_copy(dst[:, half * 512:half * 512 + 512], bank[2 + half][:, :]).then_inc(tr2c, 1)


def layer_norm(c, act_ask, act_done, n, parts, mean, cen, sq, std, out):
    v = c.eng
    for (a, z), view in parts:
        c.add(v.reduce_sum(mean[:, a:z], view, X))
    c.wait()
    c.link(v.tensor_scalar(mean, mean, 1.0 / D, None, ALU.mult))
    for (a, z), view in parts:
        c.add(v.tensor_tensor(cen[:, a:z, :], view, mean[:, a:z].unsqueeze(2).to_broadcast([P, z - a, D]),
                              ALU.subtract))
    c.wait()
    c.link(v.tensor_tensor(sq, cen, cen, ALU.mult))
    v.reduce_sum(std, sq, X).then_inc(act_ask, 1)
    v.wait_ge(act_done, n)
    c.link(v.reciprocal(std, std))
    return v.tensor_tensor(out, cen, std.unsqueeze(2).to_broadcast([P, CB, D]), ALU.mult)


HALVES = [(0, 4), (4, CB)]


def blocks_view(bank, a, z):
    return bank[:, 0:(z - a) * P].rearrange("p (b f) -> p b f", f=P)


def phase_nodes0(nc, t, i, d):
    with ExitStack() as ctx:
        (wld, xl, sA, sF, sH, sR, sO, ask, root, ln, sT, sTc, sh, shc, x1s, hst, eps_s, free, ch) = sems(
            nc, ctx, *["n_" + n for n in (
                "weights_loaded", "x_loaded", "dst_part", "agg_full", "hidden", "relu", "out", "root_asked",
                "root_done", "normed", "x1_transposed", "x1_copied", "h_products", "h_copied",
                "x1_stored", "h_stored", "eps", "chunk_done", "chain")])
        ca = region(nc, ctx, "n_region", 12600)
        cb = Carve(t["acc"][:, 2:4, :].rearrange("p a b -> p (a b)"))
        wd, w1a, w1b, w2, fc = (ca(P) for _ in range(5))
        bm, b1, fcb, gw, eps = (ca(1) for _ in range(5))
        b2r, fcbr = ca(P, parts=1), ca(P, parts=1)
        xT, agg, hid, x1T, hasc = (ca(CN) for _ in range(5))
        c3 = lambda: ca(CN).rearrange("p (b f) -> p b f", f=P)
        d3 = lambda: cb(CN).rearrange("p (b f) -> p b f", f=P)
        cen, sq, x1, hrow = d3(), d3(), d3(), d3()
        mean, std = ca(CB), ca(CB)
        start = ca(4)
        bank = t["psum"]
        ident, ones = t["ident"], t["ones"]
        acc = t["acc"]
        H = CN // 2
        block = ctx.enter_context(nc.Block())

        @block.gpsimd
        def _(pool):
            for n, (s, per) in enumerate([(free, 1), (hst, 16), (x1s, 16), (shc, 4)]):
                nc.gpsimd.memset(start[:, n:n + 1], 0.0).then_inc(s, per)

        @block.sync
        def _(sp):
            for dst, src in ((wd, i["Wm"][0:D, :]), (w1a, i["W1"][0:D, :]), (w1b, i["W1"][D:2 * D, :]), (w2, i["W2"]),
                             (fc, i["fc"]), (bm, i["bm"]), (b1, i["b1"]), (fcb, i["fcb"]), (gw, i["gw"]),
                             (b2r, i["b2row"]), (fcbr, i["fcbrow"])):
                sp.dma_start(dst, src).then_inc(wld, 16)
            with sp.Fori(0, NCH) as c:
                sp.wait_ge(free, c + 1)
                hold(sp)
                sp.dma_start(xT, i["xT"][:, bass.ds(c * CN, CN)]).then_inc(xl, 16)
                sp.wait_ge(ln, c + 1)
                hold(sp)
                sp.dma_start(d["x1"][bass.ds(c * CN, CN), :].rearrange("(b p) f -> p b f", p=P), x1).then_inc(x1s, 16)
                sp.wait_ge(shc, c * 4 + 6)
                hold(sp)
                sp.dma_start(d["h"][bass.ds(c * CN, CN), :].rearrange("(b p) f -> p b f", p=P), hrow).then_inc(hst, 16)
            sp.wait_ge(x1s, 16 * NCH + 16)
            sp.wait_ge(hst, 16 * NCH + 16)

        @block.tensor
        def _(pe):
            pe.wait_ge(wld, 11 * 16)
            with pe.Fori(0, NCH) as c:
                pe.wait_ge(xl, c * 16 + 16)
                pe.wait_ge(shc, c * 4 + 4)
                for h in range(2):
                    last = nc.tensor.matmul(bank[h][:, 0:H], wd, xT[:, h * H:(h + 1) * H], start=True, stop=True)
                last.then_inc(sA, 1)
                pe.wait_ge(sF, c + 1)
                for h in range(2):
                    nc.tensor.matmul(bank[2 + h][:, 0:H], w1a, xT[:, h * H:(h + 1) * H], start=True, stop=False)
                    last = nc.tensor.matmul(bank[2 + h][:, 0:H], w1b, agg[:, h * H:(h + 1) * H], start=False, stop=True)
                last.then_inc(sH, 1)
                pe.wait_ge(sR, c + 1)
                for h, (a, z) in enumerate(HALVES):
                    for k in range(a, z):
                        o = bank[4 + h][:, (k - a) * P:(k - a + 1) * P]
                        nc.tensor.matmul(o, hid[:, k * P:(k + 1) * P], w2, start=True, stop=False)
                        nc.tensor.matmul(o, ones[0:1, :], b2r, start=False, stop=False)
                        last = nc.tensor.matmul(o, xT[:, k * P:(k + 1) * P], ident[:, :], start=False, stop=True)
                last.then_inc(sO, 1)
                pe.wait_ge(ln, c + 1)
                for h, (a, z) in enumerate(HALVES):
                    for k in range(a, z):
                        last = nc.tensor.transpose(bank[6 + h][:, (k - a) * P:(k - a + 1) * P], x1[:, k, :], ident[:, :])
                last.then_inc(sT, 1)
                pe.wait_ge(sTc, c + 1)
                for h, (a, z) in enumerate(HALVES):
                    for k in range(a, z):
                        o = bank[4 + h][:, (k - a) * P:(k - a + 1) * P]
                        nc.tensor.matmul(o, x1T[:, k * P:(k + 1) * P], fc, start=True, stop=False)
                        nc.tensor.matmul(o, ones[0:1, :], fcbr, start=False, stop=True)
                for h in range(2):
                    nc.tensor.matmul(bank[h][:, 0:H], fc, x1T[:, h * H:(h + 1) * H], start=True, stop=True)
                for k in range(CB):
                    nc.tensor.matmul(bank[2][:, k:k + 1], x1T[:, k * P:(k + 1) * P], gw, start=True, stop=True)
                    last = nc.tensor.matmul(bank[3][:, k:k + 1], hasc[:, k * P:(k + 1) * P], ident[:, 0:1],
                                            start=True, stop=True)
                last.then_inc(sh, 1)

        @block.scalar
        def _(act):
            act.wait_ge(wld, 11 * 16)
            act.wait_ge(eps_s, 2)
            with act.Fori(0, NCH) as c:
                act.wait_ge(sH, c + 1)
                nc.scalar.activation(hid[:, 0:H], bank[2][:, 0:H], ACT.Relu, bias=b1)
                nc.scalar.activation(hid[:, H:CN], bank[3][:, 0:H], ACT.Relu, bias=b1).then_inc(sR, 1)
                act.wait_ge(ask, c + 1)
                nc.scalar.activation(std, std, ACT.Sqrt, bias=eps, scale=1.0 / D).then_inc(root, 1)
                act.wait_ge(sT, c + 1)
                for h, (a, z) in enumerate(HALVES):
                    last = nc.scalar.activation(x1T[:, a * P:z * P], bank[6 + h][:, 0:(z - a) * P], ACT.Copy)
                last.then_inc(sTc, 1)
                act.wait_ge(sh, c + 1)
                act.wait_ge(hst, c * 16 + 16)
                hold(act)
                for h, (a, z) in enumerate(HALVES):
                    nc.scalar.activation(hrow[:, a:z, :], blocks_view(bank[4 + h], a, z), ACT.Copy).then_inc(shc, 1)
                for h in range(2):
                    nc.scalar.activation(t["hT"][:, bass.ds(c * CN + h * H, H)], bank[h][:, 0:H], ACT.Identity,
                                         bias=fcb).then_inc(shc, 1)

        @block.vector
        def _(dve):
            nc.vector.memset(eps, EPS).then_inc(eps_s, 1)
            nc.vector.memset(t["hT"][:, NP:ACCW], 0.0).then_inc(eps_s, 1)
            dve.wait_ge(wld, 11 * 16)
            PER = 2 + 2 + 7
            with dve.Fori(0, NCH) as it:
                c = Count(dve, ch, it * PER)
                dve.wait_ge(sA, it + 1)
                for h in range(2):
                    at = it * CN + h * H
                    c.add(nc.vector.scalar_tensor_tensor(agg[:, h * H:(h + 1) * H], bank[h][:, 0:H], bm,
                                                         acc[:, 1, bass.ds(at, H)], ALU.add, ALU.mult))
                c.wait()
                c.add(nc.vector.tensor_tensor(agg[:, 0:H], agg[:, 0:H], acc[:, 0, bass.ds(it * CN, H)], ALU.add))
                c.add(nc.vector.tensor_tensor(agg[:, H:CN], agg[:, H:CN], acc[:, 0, bass.ds(it * CN + H, H)], ALU.add))
                c.wait()
                hold(dve)
                nc.vector.tensor_copy(hasc, acc[:, 1, bass.ds(it * CN, CN)]).then_inc(sF, 1)
                dve.wait_ge(sO, it + 1)
                dve.wait_ge(x1s, it * 16 + 16)
                layer_norm(c, ask, root, it + 1, [((a, z), blocks_view(bank[4 + h], a, z))
                                                  for h, (a, z) in enumerate(HALVES)], mean, cen, sq, std, x1
                           ).then_inc(ln, 1)
                assert c.n == PER
                dve.wait_ge(sh, it + 1)
                hold(dve)
                nc.vector.tensor_copy(t["gate_n"][:, bass.ds(it * CB, CB)], bank[2][:, 0:CB])
                nc.vector.tensor_copy(t["has_n"][:, bass.ds(it * CB, CB)], bank[3][:, 0:CB]).then_inc(free, 1)


def one_hot(nc, t, table, col, out):
    rel = table[:, bass.ds(col, GJ)].unsqueeze(2).to_broadcast([P, GJ, W])
    return nc.vector.tensor_tensor(out, t["iota_w"][:, :, :], rel, ALU.is_equal)


def phase_scores(nc, t, i, d):
    with ExitStack() as ctx:
        (zero, idxr, tp, hc, wbr, wbs, gw, amd, acd, ohs, ats) = sems(nc, ctx, *["d_" + n for n in (
            "zeroed", "idx_ready", "transposed", "columns_copied", "weights_built", "sums_done",
            "products_done", "products_masked", "windows_added", "one_hot", "scores_stored")])
        gat = sems(nc, ctx, *[f"d_gathered{q}" for q in range(NG)])
        sst = sems(nc, ctx, *[f"d_rows_stored{q}" for q in range(NG)])
        ca = region(nc, ctx, "d_region", 9000)
        G4 = GJ * P
        rows = ca(IJ * P).rearrange("p (s f) -> p s f", f=P)
        idx = ca(IJ, I32)
        hs = [ca(G4) for _ in range(2)]
        oh = [ca(GJ * W).rearrange("p (j w) -> p j w", j=GJ) for _ in range(2)]
        wb = [ca(GJ * M * W).rearrange("p (j m w) -> p j m w", j=GJ, m=M) for _ in range(2)]
        am = [ca(GJ * W).rearrange("p (j w) -> p j w", j=GJ) for _ in range(2)]
        start = ca(16)
        bank = t["psum"]
        tb, sb, pb = bank[0:2], bank[2:4], bank[4:6]
        acc = t["acc"]
        block = ctx.enter_context(nc.Block())
        CREDIT = NG

        @block.gpsimd
        def _(pool):
            for n, (s, per) in enumerate([(tp, 1), (hc, 1), (wbr, 1), (wbs, 1), (gw, 1), (amd, 1), (acd, GJ), (ats, 1)] + [(s, 4) for s in sst]):
                nc.gpsimd.memset(start[:, n:n + 1], 0.0).then_inc(s, per * CREDIT)
            gather_rows(nc, pool, t, d["h"], idx, rows, idxr, [(tp, 1), (wbs, 1)], gat, sst)

        @block.sync
        def _(sp):
            nit = iterations(sp, t)
            with sp.Fori(0, nit) as it:
                for q in range(NG):
                    sp.wait_ge(gat[q], it * 64 + 64)
                    hold(sp)
                    sp.dma_start(d["hsp"][bass.ds(it * NG + q, 1), :, :].rearrange("a p n -> (a p) n"),
                                 rows[:, q * GJ:(q + 1) * GJ, :].rearrange("p s f -> p (s f)")).then_inc(sst[q], 16)
            for q in range(NG):
                sp.wait_ge(sst[q], nit * 16 + 16)
            hold(sp)

        @block.tensor
        def _(pe):
            nit = iterations(pe, t)
            with pe.Fori(0, nit) as it:
                for q in range(NG):
                    g = it * NG
                    base = group_bases(nc, t, mybir.EngineType.PE, it, q)
                    pe.wait_ge(gat[q], it * 64 + 64)
                    pe.wait_ge(hc, g + (q - 2 + 1 + CREDIT))
                    for j in range(GJ):
                        last = nc.tensor.transpose(tb[q % 2][:, j * P:(j + 1) * P], rows[:, q * GJ + j, :],
                                                   t["ident"][:, :])
                    last.then_inc(tp, 1)
                    pe.wait_ge(wbr, g + (q + 1 + CREDIT))
                    pe.wait_ge(acd, it * (NG * GJ) + (q - 2 + 1 + CREDIT) * GJ)
                    for j in range(GJ):
                        last = nc.tensor.matmul(sb[q % 2][:, j * M * W:(j + 1) * M * W], rows[:, q * GJ + j, :],
                                                wb[q % 2][:, j, :, :].rearrange("p m w -> p (m w)"),
                                                start=True, stop=True)
                    last.then_inc(wbs, 1)
                    pe.wait_ge(hc, g + (q + 1 + CREDIT))
                    pe.wait_ge(amd, g + (q - 2 + 1 + CREDIT))
                    for j in range(GJ):
                        last = nc.tensor.matmul(pb[q % 2][:, j * W:(j + 1) * W], hs[q % 2][:, j * P:(j + 1) * P],
                                                t["hT"][:, bass.ds(base[j], W)], start=True, stop=True)
                    last.then_inc(gw, 1)

        @block.scalar
        def _(act):
            nit = iterations(act, t)
            with act.Fori(0, nit) as it:
                for q in range(NG):
                    act.wait_ge(tp, it * NG + (q + 1 + CREDIT))
                    act.wait_ge(gw, it * NG + (q - 2 + 1 + CREDIT))
                    nc.scalar.activation(hs[q % 2], tb[q % 2][:, :], ACT.Copy).then_inc(hc, 1)

        @block.vector
        def _(dve):
            nc.vector.tensor_copy(idx, t["src_col"][:, 0:IJ]).then_inc(idxr, NG)
            nc.vector.memset(t["att_col"][:, :], 0.0).then_inc(zero, 1)
            nc.vector.memset(acc[:, :, :], 0.0).then_inc(zero, 1)
            dve.wait_ge(zero, 2)

            def weights(it, q):
                g = it * NG
                col = it * IJ + q * GJ
                dve.wait_ge(amd, g + (q - 2 + 1 + CREDIT))
                one_hot(nc, t, t["rel_col"], col, oh[q % 2]).then_inc(ohs, 1)
                dve.wait_ge(ohs, g + (q + 1))
                dve.wait_ge(wbs, g + (q - 2 + 1 + CREDIT))
                nc.vector.tensor_tensor(
                    wb[q % 2], oh[q % 2].unsqueeze(2).to_broadcast([P, GJ, M, W]),
                    t["gate_col"][:, :, bass.ds(col, GJ)].rearrange("p m j -> p j m").unsqueeze(3)
                    .to_broadcast([P, GJ, M, W]), ALU.mult).then_inc(wbr, 1)

            weights(0, 0)
            nit = iterations(dve, t)
            with dve.Fori(0, nit) as it:
                for q in range(NG):
                    g = it * NG
                    col = it * IJ + q * GJ
                    base = group_bases(nc, t, mybir.EngineType.DVE, it, q)
                    weights(it, q + 1)
                    dve.wait_ge(gat[q], it * 64 + 64)
                    hold(dve)
                    nc.vector.tensor_copy(idx[:, q * GJ:(q + 1) * GJ],
                                          t["src_col"][:, bass.ds(col + IJ, GJ)]).then_inc(idxr, 1)
                    dve.wait_ge(wbs, g + (q + 1 + CREDIT))
                    for j in range(GJ):
                        dve.wait_ge(acd, it * (NG * GJ) + ((q + CREDIT) * GJ + j))
                        w = acc[:, 1:1 + M, bass.ds(base[j], W)]
                        nc.vector.tensor_tensor(w, w, sb[q % 2][:, j * M * W:(j + 1) * M * W].rearrange(
                            "p (m w) -> p m w", m=M), ALU.add).then_inc(acd, 1)
                    dve.wait_ge(gw, g + (q + 1 + CREDIT))
                    dve.wait_ge(ats, g + (q - 2 + 1 + CREDIT))
                    nc.vector.tensor_tensor(am[q % 2], pb[q % 2][:, 0:GJ * W].rearrange("p (j w) -> p j w", j=GJ),
                                            oh[q % 2], ALU.mult).then_inc(amd, 1)
                    dve.wait_ge(amd, g + (q + 1 + CREDIT))
                    nc.vector.reduce_sum(t["att_col"][:, bass.ds(col, GJ)], am[q % 2], X).then_inc(ats, 1)


def phase_sums(nc, t, i, d):
    with ExitStack() as ctx:
        (ohs, war, ws, wc, wt, acd, zero) = sems(
            nc, ctx, "f_one_hot", "f_weights_built", "f_sums_done", "f_sums_copied", "f_sums_transposed",
            "f_windows_added", "f_zeroed")
        ld = sems(nc, ctx, *[f"f_rows_loaded{q}" for q in range(NG)])
        ca = region(nc, ctx, "f_region", 6000)
        G4 = GJ * P
        rows = [ca(G4) for _ in range(NG)]
        oh = [ca(GJ * W).rearrange("p (j w) -> p j w", j=GJ) for _ in range(NG)]
        wa = [ca(GJ * W).rearrange("p (j w) -> p j w", j=GJ) for _ in range(NG)]
        sums = [ca(P) for _ in range(2)]
        start = ca(16)
        bank = t["psum"]
        into = [t["acc"][:, 0, :], t["hT"][:, :]]
        block = ctx.enter_context(nc.Block())
        CREDIT = NG

        @block.sync
        def _(sp):
            nit = iterations(sp, t)
            with sp.Fori(0, nit) as it:
                for q in range(NG):
                    sp.wait_ge(ws, it * NG + (q + 1))
                    hold(sp)
                    sp.dma_start(rows[q], d["hsp"][bass.ds(it * NG + q, 1), :, :].rearrange("a p n -> (a p) n")
                                 ).then_inc(ld[q], 16)
            sp.wait_ge(ws, nit * NG + 1)
            hold(sp)
            sp.dma_start(rows[0], d["hsp"][0, :, :]).then_inc(ld[0], 16)

        @block.tensor
        def _(pe):
            nit = iterations(pe, t)

            def sum_rows(it, q):
                pe.wait_ge(ld[q % NG], it * 16 + 16 * (q // NG + 1))
                pe.wait_ge(war, it * NG + (q + 1 + CREDIT))
                pe.wait_ge(wc, it * NG + (q - 2 + 1 + CREDIT))
                for j in range(GJ):
                    last = nc.tensor.matmul(bank[q % 2][j * W:(j + 1) * W, 0:P], wa[q % NG][:, j, :],
                                            rows[q % NG][:, j * P:(j + 1) * P], start=True, stop=True)
                last.then_inc(ws, 1)

            sum_rows(0, 0)
            with pe.Fori(0, nit) as it:
                for q in range(NG):
                    g = it * NG
                    sum_rows(it, q + 1)
                    pe.wait_ge(wc, g + (q + 1 + CREDIT))
                    pe.wait_ge(acd, it * (NG * GJ) + (q - 2 + 1 + CREDIT) * GJ)
                    nc.tensor.transpose(bank[2 + q % 2][:, 0:P], sums[q % 2], t["ident"][:, :]).then_inc(wt, 1)

        @block.scalar
        def _(act):
            nit = iterations(act, t)
            with act.Fori(0, nit) as it:
                for q in range(NG):
                    act.wait_ge(ws, it * NG + (q + 1 + CREDIT))
                    act.wait_ge(wt, it * NG + (q - 2 + 1 + CREDIT))
                    nc.scalar.activation(sums[q % 2], bank[q % 2][:, 0:P], ACT.Copy).then_inc(wc, 1)

        @block.gpsimd
        def _(pool):
            for n, (s, per) in enumerate([(ohs, 1), (war, 1), (ws, 1), (wc, 1), (wt, 1), (acd, GJ)]):
                nc.gpsimd.memset(start[:, n:n + 1], 0.0).then_inc(s, per * CREDIT)
            nit = iterations(pool, t)
            def weights(it, q):
                pool.wait_ge(ohs, it * NG + (q + 1 + CREDIT))
                pool.wait_ge(ws, it * NG + (q - NG + 1 + CREDIT))
                nc.gpsimd.tensor_tensor(
                    wa[q % NG], oh[q % NG],
                    t["att_col"][:, bass.ds(it * IJ + q * GJ, GJ)].unsqueeze(2).to_broadcast([P, GJ, W]),
                    ALU.mult).then_inc(war, 1)

            weights(0, 0)
            with pool.Fori(0, nit) as it:
                for q in range(NG):
                    weights(it, q + 1)

        @block.vector
        def _(dve):
            nc.vector.memset(t["hT"][:, :], 0.0).then_inc(zero, 1)
            dve.wait_ge(zero, 1)
            for q in range(2):
                one_hot(nc, t, t["rel_col"], q * GJ, oh[q]).then_inc(ohs, 1)
            nit = iterations(dve, t)
            with dve.Fori(0, nit) as it:
                for q in range(NG):
                    base = group_bases(nc, t, mybir.EngineType.DVE, it, q)
                    dve.wait_ge(war, it * NG + (q - 2 + 1 + CREDIT))
                    one_hot(nc, t, t["rel_col"], it * IJ + (q + 2) * GJ, oh[(q + 2) % NG]).then_inc(ohs, 1)
                    dve.wait_ge(wt, it * NG + (q + 1 + CREDIT))
                    for j in range(GJ):
                        dve.wait_ge(acd, it * (NG * GJ) + ((q + CREDIT) * GJ + j - 1))
                        w = into[j % 2][:, bass.ds(base[j], W)]
                        nc.vector.tensor_tensor(w, w, bank[2 + q % 2][:, j * W:(j + 1) * W], ALU.add).then_inc(acd, 1)


def phase_nodes1(nc, t, i, d, out):
    with ExitStack() as ctx:
        (wld, wp, wc, gs, cf, hl, xl, su, sr, sT, su_v, mx, mxc, ask, root, ln, ost, eps_s, ch) = sems(
            nc, ctx, *["g_" + n for n in (
                "weights_loaded", "weight_products", "weights_copied", "gate", "coefficients", "h_loaded", "x1_loaded",
                "out_product", "relu", "transposed", "transposed_read", "rest_mixed", "rest_chain", "root_asked",
                "root_done", "normed", "stored", "eps", "chain")])
        ca = region(nc, ctx, "g_region", 12600)
        att, rel = ca(M * P), ca(M * P)
        o1, o2 = ca(P), ca(P)
        w = [ca(P) for _ in range(1 + M)]
        ob, gb, eps = ca(1), ca(1), ca(1)
        gate, cu, chh, cx = (ca(NBLK) for _ in range(4))
        u = ca(CN)
        c3 = lambda: ca(CN).rearrange("p (b f) -> p b f", f=P)
        h, x1, v, cen, sq, y = (c3() for _ in range(6))
        rest = [c3() for _ in range(1)][0]
        mean, std = ca(CB), ca(CB)
        start = ca(5)
        bank = t["psum"]
        ident = t["ident"]
        acc = t["acc"]
        H = CN // 2
        block = ctx.enter_context(nc.Block())

        @block.sync
        def _(sp):
            for dst, src in ((att.rearrange("p (m f) -> p m f", m=M), i["attT"].rearrange("m j d -> j m d")),
                             (rel.rearrange("p (m f) -> p m f", m=M), i["relT"].rearrange("m j d -> j m d")),
                             (o1, i["outW"][0:D, :]), (o2, i["outW"][D:2 * D, :]), (ob, i["outb"]),
                             (gb, i["gb"].partition_broadcast(P))):
                sp.dma_start(dst, src).then_inc(wld, 16)
            with sp.Fori(0, NCH) as c:
                sp.wait_ge(mx, c + 1)
                hold(sp)
                sp.dma_start(h, d["h"][bass.ds(c * CN, CN), :].rearrange("(b p) f -> p b f", p=P)).then_inc(hl, 16)
                sp.dma_start(x1, d["x1"][bass.ds(c * CN, CN), :].rearrange("(b p) f -> p b f", p=P)).then_inc(xl, 16)
                sp.wait_ge(ln, c + 1)
                hold(sp)
                sp.dma_start(out[bass.ds(c * CN, CN), :].rearrange("(b p) f -> p b f", p=P), y).then_inc(ost, 16)
            sp.wait_ge(ost, 16 * NCH + 16)

        @block.tensor
        def _(pe):
            pe.wait_ge(wld, 6 * 16)
            for k in range(M):
                nc.tensor.matmul(bank[0][:, 0:P], att[:, k * P:(k + 1) * P], o1, start=(k == 0), stop=(k == M - 1))
            for m in range(M):
                last = nc.tensor.matmul(bank[0][:, (1 + m) * P:(2 + m) * P], rel[:, m * P:(m + 1) * P], o2,
                                        start=True, stop=True)
            last.then_inc(wp, 1)
            pe.wait_ge(wc, 1 + M)
            with pe.Fori(0, NCH) as c:
                pe.wait_ge(sr, c + 1)
                for s in range(2):
                    nc.tensor.matmul(bank[1 + s][:, 0:H], w[0], t["hT"][:, bass.ds(c * CN + s * H, H)],
                                     start=True, stop=False)
                    for k in range(1 + M):
                        last = nc.tensor.matmul(bank[1 + s][:, 0:H], w[k], acc[:, k, bass.ds(c * CN + s * H, H)],
                                                start=False, stop=(k == M))
                last.then_inc(su, 1)
                pe.wait_ge(sr, c + 2)
                pe.wait_ge(su_v, c + 1)
                for s, (a, z) in enumerate(HALVES):
                    for k in range(a, z):
                        last = nc.tensor.transpose(bank[3 + s][:, (k - a) * P:(k - a + 1) * P], u[:, k * P:(k + 1) * P],
                                                   ident[:, :])
                last.then_inc(sT, 1)

        @block.scalar
        def _(act):
            act.wait_ge(wld, 6 * 16)
            nc.scalar.activation(gate, t["gate_n"][:, :], ACT.Sigmoid, bias=gb).then_inc(gs, 1)
            act.wait_ge(wp, 1)
            for k in range(1 + M):
                nc.scalar.activation(w[k], bank[0][:, k * P:(k + 1) * P], ACT.Copy, scale=1.0 / 3.0).then_inc(wc, 1)
            act.wait_ge(eps_s, 1)
            with act.Fori(0, NCH) as c:
                act.wait_ge(su, c + 1)
                act.wait_ge(sT, c + 1)
                nc.scalar.activation(u[:, 0:H], bank[1][:, 0:H], ACT.Relu, bias=ob)
                nc.scalar.activation(u[:, H:CN], bank[2][:, 0:H], ACT.Relu, bias=ob).then_inc(sr, 1)
                act.wait_ge(ask, c + 1)
                nc.scalar.activation(std, std, ACT.Sqrt, bias=eps, scale=1.0 / D).then_inc(root, 1)

        @block.gpsimd
        def _(pool):
            for n, (s, per) in enumerate([(mx, 1), (sr, 1), (sT, 1), (su_v, 1), (ost, 16)]):
                nc.gpsimd.memset(start[:, n:n + 1], 0.0).then_inc(s, per)
            pool.wait_ge(cf, 1)
            with pool.Fori(0, NCH) as c:
                cc = Count(pool, mxc, c * 2)
                pool.wait_ge(hl, c * 16 + 16)
                pool.wait_ge(xl, c * 16 + 16)
                pool.wait_ge(su_v, c + 1)
                cc.add(nc.gpsimd.tensor_tensor(rest, h, chh[:, bass.ds(c * CB, CB)].unsqueeze(2)
                                               .to_broadcast([P, CB, P]), ALU.mult))
                cc.add(nc.gpsimd.tensor_tensor(x1, x1, cx[:, bass.ds(c * CB, CB)].unsqueeze(2)
                                               .to_broadcast([P, CB, P]), ALU.mult))
                cc.wait()
                nc.gpsimd.tensor_tensor(rest, rest, x1, ALU.add).then_inc(mx, 1)

        @block.vector
        def _(dve):
            nc.vector.memset(eps, EPS).then_inc(eps_s, 1)
            dve.wait_ge(gs, 1)
            c0 = Count(dve, ch)
            c0.link(nc.vector.tensor_tensor(cu, gate, t["has_n"][:, :], ALU.mult))
            c0.add(nc.vector.tensor_tensor(chh, gate, cu, ALU.subtract))
            c0.add(nc.vector.tensor_scalar(cx, gate, -1.0, 2.0, ALU.mult, ALU.add))
            c0.wait()
            nc.vector.memset(mean, 0.0).then_inc(cf, 1)
            PRE, PER = 3, 2 + 5
            with dve.Fori(0, NCH) as it:
                c = Count(dve, ch, it * PER + PRE)
                dve.wait_ge(sT, it + 2)
                dve.wait_ge(mx, it + 2)
                for s, (a, z) in enumerate(HALVES):
                    c.add(nc.vector.tensor_tensor(v[:, a:z, :], blocks_view(bank[3 + s], a, z),
                                                  cu[:, bass.ds(it * CB + a, z - a)].unsqueeze(2)
                                                  .to_broadcast([P, z - a, P]), ALU.mult))
                c.wait()
                nc.vector.tensor_tensor(v, v, rest, ALU.add).then_inc(su_v, 1)
                dve.wait_ge(su_v, it + 2)
                dve.wait_ge(ost, it * 16 + 16)
                layer_norm(c, ask, root, it + 1, [((0, CB), v)], mean, cen, sq, std, y).then_inc(ln, 1)
                assert c.n == PER


def build(nc, i, out):
    def dram(name, shape, dt=F32):
        return nc.dram_tensor("d_" + name, shape, dt).ap()

    d = dict(tiles=dram("tiles", [TC * P, TW]), B=dram("src_product", [NP, P]),
             valid=dram("valid", [JP * P]), keep=dram("keep", [JP * P]), stop=dram("stop", [JP * P]),
             reset=dram("reset", [JP * P], BF16), w9=dram("w9", [9, JP * P], BF16), ww9=dram("ww9", [9, P], BF16),
             base=dram("base", [JP], I32), gates=dram("gates", [JP, M * P]),
             flat=dram("flat", [M, JP * P]), wflat=dram("wflat", [M, JP * P]),
             x1=dram("x1", [NP, P]), h=dram("h", [NP, P]), hsp=dram("rows", [JP // GJ, P, GJ * P]))
    with ExitStack() as ctx:
        t = tensors(nc, ctx)
        phase_tables(nc, t, i, d)
        phase_layer0(nc, t, i, d)
        phase_softmax(nc, t, i, d, True)
        phase_nodes0(nc, t, i, d)
        phase_scores(nc, t, i, d)
        phase_softmax(nc, t, i, d, False)
        phase_sums(nc, t, i, d)
        phase_nodes1(nc, t, i, d, out)


def kernel(x, src, dst, edge_attr_64, edge_weight, L0_gnn_Wm, L0_gnn_bm, L0_gnn_W1, L0_gnn_b1, L0_gnn_W2, L0_gnn_b2,
           L1_gnn_node_att_W, L1_gnn_rel_att_W, L1_gnn_rel_att_W1, L1_gnn_rel_att_b1, L1_gnn_rel_att_W2,
           L1_gnn_rel_att_b2, L1_gnn_node_fc_W, L1_gnn_node_fc_b, L1_gnn_edge_fc_W, L1_gnn_edge_fc_b,
           L1_gnn_out_fc_W, L1_gnn_out_fc_b, L1_gnn_gate_W, L1_gnn_gate_b):
    import numpy as np
    import concourse.bacc as bacc
    from concourse.bass_utils import run_bass_kernel_spmd

    a = lambda v: np.ascontiguousarray(v)
    f32, i32 = np.float32, np.int32
    pad = TC * P * P - E
    col, row = (lambda v: a(v).reshape(-1, 1)), (lambda v: a(v).reshape(1, -1))
    ea = np.concatenate([a(edge_attr_64), np.zeros((JP * P - E, DE), f32)])
    arrays = dict(
        dst=np.concatenate([np.full(1, -1, i32), a(dst), np.full(pad + 1, PAD_DST, i32)]),
        src=np.concatenate([a(src), np.zeros(pad, i32)]),
        w=np.concatenate([a(edge_weight), np.zeros(pad, f32)]),
        xT=a(np.concatenate([a(x), np.zeros((NP - N, D), f32)]).T),
        eaT=a(ea.reshape(JP // GJ, GJ * P, DE).transpose(0, 2, 1)),
        Wm=a(L0_gnn_Wm), bm=col(L0_gnn_bm), W1=a(L0_gnn_W1), b1=col(L0_gnn_b1), W2=a(L0_gnn_W2), b2row=row(L0_gnn_b2),
        weT=a(np.asarray(L1_gnn_edge_fc_W).T), be=col(L1_gnn_edge_fc_b), w1=a(L1_gnn_rel_att_W1),
        b1T=a(np.asarray(L1_gnn_rel_att_b1).T), w2T=a(np.asarray(L1_gnn_rel_att_W2).T), b2=a(L1_gnn_rel_att_b2),
        fc=a(L1_gnn_node_fc_W), fcb=col(L1_gnn_node_fc_b), fcbrow=row(L1_gnn_node_fc_b),
        attT=a(np.asarray(L1_gnn_node_att_W).transpose(0, 2, 1)),
        relT=a(np.asarray(L1_gnn_rel_att_W).transpose(0, 2, 1)),
        outW=a(L1_gnn_out_fc_W), outb=col(L1_gnn_out_fc_b), gw=a(L1_gnn_gate_W), gb=a(L1_gnn_gate_b))
    nc = bacc.Bacc("TRN2", target_bir_lowering=False, num_devices=1)
    i = {k: nc.dram_tensor(k, v.shape, mybir.dt.from_np(v.dtype), kind="ExternalInput").ap() for k, v in arrays.items()}
    out = nc.dram_tensor("out", [NP, D], F32, kind="ExternalOutput").ap()
    build(nc, i, out)
    r = run_bass_kernel_spmd(nc, [arrays], core_ids=[0])
    return r.results[0]["out"][:N]
```

```python
from contextlib import ExitStack

import concourse.bass as bass
from concourse import mybir

F32 = mybir.dt.float32
I32 = mybir.dt.int32
BF16 = mybir.dt.bfloat16
F32R = mybir.dt.float32r
ALU = mybir.AluOpType
ACT = mybir.ActivationFunctionType
X = mybir.AxisListType.X

P = 128
N, E, D, DE, M = 6250, 100000, 128, 64, 3
NT = -(-E // P)
TC = -(-NT // P)
W = 32
JC = 8
JP = JC * P
GJ = 4
NG = 4
IJ = GJ * NG
NBLK = -(-N // P)
CB = 7
CN = CB * P
NCH = NBLK // CB
NP = NBLK * P
ACCW = NP + W
BIG = float(2.0 ** 100)
PAD_DST = 8191
SRC, DST, WGT, ST, EN, FIRST, START = 0, P, 2 * P, 3 * P, 4 * P, 5 * P, 5 * P + 1
TW = 5 * P + 8
FLAT = JP * P // P
EPS = 1e-5
MAXIT = -(-(NT + -(-N // W)) // IJ)
assert MAXIT * IJ + IJ <= JP and NBLK == CB * NCH and NT < PAD_DST


class Count:

    def __init__(self, eng, sem, base=0):
        self.eng, self.sem, self.base, self.n = eng, sem, base, 0

    def add(self, ins):
        self.n += 1
        ins.then_inc(self.sem, 1)
        return self.n

    def wait(self, n=None):
        self.eng.wait_ge(self.sem, self.base + (self.n if n is None else n))

    def link(self, ins):
        self.add(ins)
        self.wait()


def split3(c, x, rest, parts):
    v = c.eng
    c.link(v.tensor_copy(parts[0], x))
    c.link(v.tensor_tensor(rest, x, parts[0], ALU.subtract))
    c.link(v.tensor_copy(parts[1], rest))
    c.link(v.tensor_tensor(rest, rest, parts[1], ALU.subtract))
    c.link(v.tensor_copy(parts[2], rest))


def sems(nc, ctx, *names):
    return [ctx.enter_context(nc.semaphore(n)) for n in names]


def tensors(nc, ctx):
    def sb(name, shape, dt=F32):
        return ctx.enter_context(nc.sbuf_tensor(name, shape, dt))

    t = {}
    t["ident"] = sb("ident", [P, P])
    t["ones"] = sb("ones", [P, P])
    t["iota_w"] = sb("iota_w", [P, GJ, W])
    t["base_row"] = sb("base_row", [1, JP + IJ], I32)
    t["nit"] = sb("nit", [P, 1], I32)
    t["src_col"] = sb("src_col", [P, JP + IJ], I32)
    t["rel_col"] = sb("rel_col", [P, JP])
    t["end_col"] = sb("end_col", [P, JP])
    t["tile_of_job"] = sb("tile_of_job", [P, JC], I32)
    t["hT"] = sb("hT", [P, ACCW])
    t["has_n"] = sb("has_n", [P, NBLK])
    t["gate_n"] = sb("gate_n", [P, NBLK])
    t["acc"] = sb("acc", [P, 4, ACCW])
    t["gate_col"] = sb("gate_col", [P, M, JP])
    t["att_col"] = sb("att_col", [P, JP])
    t["psum"] = [ctx.enter_context(nc.psum_tensor(f"bank{i}", [P, 512], F32)) for i in range(8)]
    return t


def region(nc, ctx, name, words):
    return Carve(ctx.enter_context(nc.sbuf_tensor(name, [P, words], F32))[:, :])


class Carve:

    def __init__(self, region):
        self.region, self.at = region, 0

    def __call__(self, cols, dt=F32, parts=P):
        words = cols if dt in (F32, I32) else -(-cols // 2)
        ap = self.region[0:parts, self.at:self.at + words]
        self.at += words
        assert self.at <= self.region.shape[1], self.at
        return ap if dt == F32 else ap.bitcast(dt)


def phase_tables(nc, t, i, d):
    with ExitStack() as ctx:
        (ld, ldw, cst, ch, stt, peS, peR, jr, peT, cpT, flat, back, pb, bcp) = sems(
            nc, ctx, "a_loaded", "a_ws_loaded", "a_consts", "a_chain", "a_tiles_stored",
            "a_prefix_done", "a_rows_done", "a_jobs_gathered", "a_transposed", "a_transposed_copied",
            "a_flat_stored", "a_base_moved", "a_b_product", "a_b_copied")
        ldx = sems(nc, ctx, "a_x_even_loaded", "a_x_odd_loaded")
        bst = sems(nc, ctx, "a_b_even_stored", "a_b_odd_stored")
        ca = region(nc, ctx, "a_region", 12600)
        v3 = lambda ap, a: ap.rearrange("p (a b) -> p a b", a=a)
        dI = v3(ca(TC * P, I32), TC)
        prevI = v3(ca(TC * P, I32), TC)
        nextI = v3(ca(TC * P, I32), TC)
        srcI = v3(ca(TC * P, I32), TC)
        accf = t["acc"][:, :, :].rearrange("p a b -> p (a b)")
        cb = Carve(accf)
        rec = v3(cb(TC * TW), TC)
        job = v3(cb(JC * TW), JC)
        rel = v3(cb(JP), JC)
        valid = v3(cb(JP), JC)
        relend = v3(cb(JP), JC)
        keep = v3(cb(JP), JC)
        stop = v3(cb(JP), JC)
        rst = v3(cb(JP, BF16), JC)
        wpart = [v3(ca(JP, BF16), JC) for _ in range(3)]
        wrest = v3(cb(JP), JC)
        ww, wwrest = ca(P, parts=1), ca(P, parts=1)
        wwpart = [ca(P, BF16, parts=1) for _ in range(3)]
        zero = ca(M * P)
        srow = cb(TC * P)
        cmp = cb(TC * P)
        upper = ca(P)
        tnum = ca(TC)
        jnum = ca(JC)
        km, kcum, kall = ca(TC), ca(TC), ca(1)
        kmI = ca(TC, I32)
        tj = ca(JC)
        base = ca(JC)
        tmp8 = ca(JC)
        baseI = ca(P, I32, parts=JC)
        ws = ca(P)
        xr = [ca(CN), ca(CN)]
        bo = [ca(CN), ca(CN)]
        bank = t["psum"]
        ident, ones = t["ident"], t["ones"]
        block = ctx.enter_context(nc.Block())
        NTR = 5

        @block.gpsimd
        def _(pool):
            c = Count(pool, cst)
            c.add(nc.gpsimd.memset(ident[:, :], 0.0))
            c.add(nc.gpsimd.memset(ones[:, :], 1.0))
            c.wait()
            c.add(nc.gpsimd.affine_select(out=ident[:, :], in_=ident[:, :], compare_op=ALU.not_equal, fill=1.0,
                                          base=0, pattern=[[-1, P]], channel_multiplier=1))
            c.add(nc.gpsimd.affine_select(out=upper, in_=ones[:, :], compare_op=ALU.is_gt, fill=0.0,
                                          base=0, pattern=[[1, P]], channel_multiplier=-1))
            c.add(nc.gpsimd.iota(tnum, [[P, TC]], base=0, channel_multiplier=1, allow_small_or_imprecise_dtypes=True))
            c.add(nc.gpsimd.iota(jnum, [[P, JC]], base=0, channel_multiplier=1, allow_small_or_imprecise_dtypes=True))
            c.add(nc.gpsimd.iota(t["iota_w"][:, :, :], [[0, GJ], [1, W]], base=0, channel_multiplier=0,
                                 allow_small_or_imprecise_dtypes=True))
            c.add(nc.gpsimd.memset(t["src_col"][:, JP:], 0))
            c.add(nc.gpsimd.memset(t["base_row"][:, JP:], 0))
            assert c.n == 9
            pool.wait_ge(stt, 16)
            pool.wait_ge(ch, CH_TJ)
            for k in range(JC):
                pool.indirect_dma_start(job[:, k, :], None, d["tiles"],
                                        bass.IndirectOffsetOnAxis(t["tile_of_job"][:, k:k + 1], 0)).then_inc(jr, 16)

        @block.sync
        def _(sp):
            def tiles(ap, off):
                return ap[off:off + TC * P * P].rearrange("(c p e) -> p c e", p=P, e=P)
            sp.dma_start(dI, tiles(i["dst"], 1)).then_inc(ld, 16)
            sp.dma_start(prevI, tiles(i["dst"], 0)).then_inc(ld, 16)
            sp.dma_start(nextI, tiles(i["dst"], 2)).then_inc(ld, 16)
            sp.dma_start(srcI, tiles(i["src"], 0)).then_inc(ld, 16)
            sp.dma_start(rec[:, :, WGT:WGT + P], tiles(i["w"], 0)).then_inc(ld, 16)
            sp.dma_start(ws, i["Wm"][D:2 * D, :]).then_inc(ldw, 16)
            for c in range(2):
                sp.dma_start(xr[c], i["xT"][:, c * CN:(c + 1) * CN]).then_inc(ldx[c % 2], 16)
            sp.dma_start(ww, i["Wm"][2 * D:2 * D + 1, :]).then_inc(ldw, 16)
            sp.wait_ge(ch, CH_REC)
            sp.dma_start(d["tiles"].rearrange("(c p) w -> p c w", p=P), rec).then_inc(stt, 16)
            sp.dma_start(d["gates"][NT // IJ * IJ:TC * P, :], zero[0:TC * P - NT // IJ * IJ, :]).then_inc(flat, 16)
            for a in range(3):
                for b in range(3):
                    sp.dma_start(d["ww9"][3 * a + b:3 * a + b + 1, :], wwpart[a]).then_inc(flat, 16)
            for c in range(NCH):
                sp.wait_ge(bcp, c + 1)
                sp.dma_start(d["B"][c * CN:(c + 1) * CN, :].rearrange("(b p) f -> p b f", p=P),
                             v3(bo[c % 2], CB)).then_inc(bst[c % 2], 16)
                if c + 2 < NCH:
                    sp.wait_ge(pb, c + 1)
                    sp.dma_start(xr[c % 2], i["xT"][:, (c + 2) * CN:(c + 3) * CN]).then_inc(ldx[c % 2], 16)
            sp.wait_ge(ch, CH_BASE)
            sp.dma_start(d["base"].rearrange("(c p) -> c p", p=P), baseI).then_inc(back, 16)
            sp.wait_ge(back, 16)
            sp.dma_start(t["base_row"][0:1, 0:JP], d["base"].rearrange("(a n) -> a n", a=1)).then_inc(back, 16)
            jrow = lambda ap: ap.rearrange("(c p e) -> p c e", p=P, e=P)
            sp.dma_start(jrow(d["valid"]), valid).then_inc(flat, 16)
            sp.dma_start(jrow(d["keep"]), keep).then_inc(flat, 16)
            sp.dma_start(jrow(d["stop"]), stop).then_inc(flat, 16)
            sp.dma_start(jrow(d["reset"]), rst).then_inc(flat, 16)
            sp.wait_ge(ch, CH_FLAGS)
            for b in range(3):
                sp.dma_start(jrow(d["w3"][b, :]), wpart[b]).then_inc(flat, 16)
            sp.wait_ge(flat, (4 + 3 + 9 + 1) * 16)
            sp.wait_ge(bst[0], 16 * (NCH - NCH // 2))
            sp.wait_ge(bst[1], 16 * (NCH // 2))
            sp.wait_ge(back, 32)

        @block.vector
        def _(dve):
            c = Count(dve, ch)
            dve.wait_ge(ld, 5 * 16)
            c.add(nc.vector.tensor_copy(rec[:, :, DST:DST + P], dI))
            c.add(nc.vector.tensor_copy(rec[:, :, SRC:SRC + P], srcI))
            c.add(nc.vector.tensor_tensor(rec[:, :, ST:ST + P], dI, prevI, ALU.not_equal))
            c.add(nc.vector.tensor_tensor(rec[:, :, EN:EN + P], dI, nextI, ALU.not_equal))
            c.wait()
            dd = rec[:, :, DST:DST + P]
            real = v3(cmp, TC)
            c.link(nc.vector.scalar_tensor_tensor(real, dd, float(PAD_DST), dd, ALU.is_lt, ALU.mult))
            c.link(nc.vector.reduce_max(km, real, X))
            c.link(nc.vector.tensor_tensor(km, km, rec[:, :, DST], ALU.subtract))
            c.link(nc.vector.tensor_scalar(kmI, km, 0.0, None, ALU.max))
            c.link(nc.vector.tensor_single_scalar(kmI, kmI, 5, ALU.arith_shift_right))
            c.link(nc.vector.tensor_copy(km, kmI))
            c.add(nc.vector.memset(kcum[:, 0:1], 0.0))
            dve.wait_ge(cst, 9)
            c.add(nc.vector.tensor_tensor_scan(kcum[:, 1:TC], ones[:, 0:TC - 1], km[:, 0:TC - 1], 0.0,
                                               ALU.mult, ALU.add))
            c.link(nc.vector.reduce_sum(kall, km, X))
            assert c.n == CH_KM
            dve.wait_ge(peS, 1)
            c.add(nc.vector.tensor_tensor(rec[:, :, START], bank[0][:, 0:TC], tnum, ALU.add))
            c.link(nc.vector.tensor_copy(rec[:, :, FIRST], rec[:, :, DST]))
            c.add(nc.vector.tensor_copy(rec[:, :, START + 1:TW], rec[:, :, DST:DST + TW - START - 1]))
            c.add(nc.vector.memset(zero, 0.0))
            dve.wait_ge(ldw, 32)
            split3(c, ww, wwrest, wwpart)
            assert c.n == CH_REC
            c.link(nc.vector.tensor_scalar(t["nit"][:, :], bank[1][:, 0:1], float(NT + IJ - 1), None, ALU.add))
            c.link(nc.vector.tensor_single_scalar(t["nit"][:, :], t["nit"][:, :], 4, ALU.arith_shift_right))
            dve.wait_ge(peR, 1)
            c.add(nc.vector.tensor_copy(srow[:, 0:4 * P], bank[2][:, :]))
            c.link(nc.vector.tensor_copy(srow[:, 4 * P:TC * P], bank[3][:, 0:(TC - 4) * P]))
            for k in range(JC):
                c.link(nc.vector.tensor_scalar(cmp, srow, jnum[:, k:k + 1], 0.0, ALU.is_le, ALU.add,
                                               accum_out=tj[:, k:k + 1]))
            c.link(nc.vector.tensor_scalar(t["tile_of_job"][:, :], tj, -1.0, None, ALU.add))
            assert c.n == CH_TJ
            dve.wait_ge(jr, 16 * JC)
            c.link(nc.vector.tensor_tensor(tmp8, jnum, job[:, :, START], ALU.subtract))
            c.link(nc.vector.scalar_tensor_tensor(base, tmp8, float(W), job[:, :, FIRST], ALU.mult, ALU.add))
            c.link(nc.vector.tensor_scalar(base, base, float(N), None, ALU.min))
            c.link(nc.vector.tensor_tensor(rel, job[:, :, DST:DST + P],
                                           base.unsqueeze(2).to_broadcast([P, JC, P]), ALU.subtract))
            c.link(nc.vector.tensor_scalar(valid, rel, 0.0, None, ALU.is_ge))
            c.link(nc.vector.scalar_tensor_tensor(valid, rel, float(W), valid, ALU.is_lt, ALU.mult))
            c.add(nc.vector.tensor_tensor(stop, job[:, :, EN:EN + P], valid, ALU.mult))
            c.link(nc.vector.tensor_tensor(keep, job[:, :, ST:ST + P], valid, ALU.mult))
            c.add(nc.vector.tensor_scalar(keep, keep, -1.0, 1.0, ALU.mult, ALU.add))
            c.add(nc.vector.tensor_scalar(rst, job[:, :, ST:ST + P], -BIG, None, ALU.mult))
            c.link(nc.vector.scalar_tensor_tensor(relend, rel, 1.0, job[:, :, EN:EN + P], ALU.add, ALU.mult))
            c.link(nc.vector.tensor_scalar(relend, relend, -1.0, None, ALU.add))
            dve.wait_ge(peT, 1)
            c.add(nc.vector.tensor_copy(baseI, bank[0][0:JC, 0:P]))
            assert c.n == CH_BASE
            split3(c, job[:, :, WGT:WGT + P], wrest, wpart)
            assert c.n == CH_FLAGS
            for n, dst in enumerate((t["src_col"], t["rel_col"], t["end_col"])):
                for half in range(2):
                    dve.wait_ge(peT, 2 + 2 * n + half)
                    nc.vector.tensor_copy(dst[:, half * 512:half * 512 + 512],
                                          bank[2 + half][:, :]).then_inc(cpT, 1)

        @block.tensor
        def _(pe):
            pe.wait_ge(cst, 9)
            def product(c):
                pe.wait_ge(ldx[c % 2], 16 * (c // 2 + 1))
                if c:
                    pe.wait_ge(bcp, c)
                for b in range(CB):
                    o = bank[4 + b // 4][:, b % 4 * P:b % 4 * P + P]
                    last = nc.tensor.matmul(o, xr[c % 2][:, b * P:(b + 1) * P], ws, start=True, stop=True)
                last.then_inc(pb, 1)
            pe.wait_ge(ldw, 32)
            product(0)
            pe.wait_ge(ch, CH_KM)
            nc.tensor.matmul(bank[0][:, 0:TC], upper, km, start=True, stop=False)
            nc.tensor.matmul(bank[0][:, 0:TC], ones[:, :], kcum, start=False, stop=True)
            nc.tensor.matmul(bank[1][:, 0:1], ones[:, :], kall, start=True, stop=True).then_inc(peS, 1)
            pe.wait_ge(ch, CH_KM + 2)
            for k in range(TC):
                last = nc.tensor.matmul(bank[2 + k // 4][:, k % 4 * P:k % 4 * P + P],
                                        rec[:, k, START:START + 1].to_broadcast([P, P]), ident[:, :],
                                        start=True, stop=True)
            last.then_inc(peR, 1)
            for c in range(1, NCH):
                product(c)
            pe.wait_ge(ch, CH_TJ + 3)
            nc.tensor.matmul(bank[0][0:JC, 0:P], base, ident[:, :], start=True, stop=True).then_inc(peT, 1)
            pe.wait_ge(ch, CH_BASE)
            for n, field in enumerate((job[:, :, SRC:SRC + P], rel, relend)):
                for half in range(2):
                    if n:
                        pe.wait_ge(cpT, 2 * n - 1 + half)
                    for k in range(4):
                        last = nc.tensor.matmul(bank[2 + half][:, k * P:(k + 1) * P], field[:, half * 4 + k, :],
                                                ident[:, :], start=True, stop=True)
                    last.then_inc(peT, 1)

        @block.scalar
        def _(act):
            for c in range(NCH):
                act.wait_ge(pb, c + 1)
                if c >= 2:
                    act.wait_ge(bst[c % 2], 16 * (c // 2))
                nc.scalar.activation(bo[c % 2][:, 0:4 * P], bank[4][:, :], ACT.Copy)
                nc.scalar.activation(bo[c % 2][:, 4 * P:CN], bank[5][:, 0:CN - 4 * P], ACT.Copy).then_inc(bcp, 1)


CH_KM = 13
CH_REC = CH_KM + 3 + 1 + 5
CH_TJ = CH_REC + 2 + 2 + JC + 1
CH_BASE = CH_TJ + 12 + 1
CH_FLAGS = CH_BASE + 5


def group_bases(nc, t, eng_type, it, q):
    _, v = nc.values_load_multi_w_load_instructions(
        t["base_row"][0:1, bass.ds(it * IJ + q * GJ, GJ)], engines=[eng_type], min_val=0, max_val=N,
        skip_runtime_bounds_check_because="the table's entries are held to at most N when it is made")
    return v


def iteration_bases(nc, t, eng_type, it):
    _, v = nc.values_load_multi_w_load_instructions(
        t["base_row"][0:1, bass.ds(it * IJ, IJ)], engines=[eng_type], min_val=0, max_val=N,
        skip_runtime_bounds_check_because="the table's entries are held to at most N when it is made")
    return v


def iterations(eng, t):
    return eng.value_load(t["nit"][0:1, 0:1], min_val=NT // IJ, max_val=MAXIT)


def gather_rows(nc, pool, t, table, idx, rows, idx_ready, slot_free, gathered, stored=None, ahead=False):
    nit = iterations(pool, t)

    def group(it, q):
        pool.wait_ge(idx_ready, it * NG + (q + 1))
        for sem, per in slot_free:
            pool.wait_ge(sem, it * (NG * per) + (q + 1) * per)
        if stored:
            pool.wait_ge(stored[q], it * 16 + 16)
        hold(pool)
        for j in range(GJ):
            s = q * GJ + j
            pool.indirect_dma_start(rows[:, s, :], None, table,
                                    bass.IndirectOffsetOnAxis(idx[:, s:s + 1], 0)).then_inc(gathered[q], 16)

    with pool.Fori(0, nit) as it:
        for q in range(NG):
            group(it, q)
    if ahead:
        group(nit, 0)


def phase_layer0(nc, t, i, d):
    with ExitStack() as ctx:
        (wld, pre, pre2, zero, zero9, idxr, p1, scd, t2, ehd, st, pk, pkc, ex, acd, es, tm, ra, rd, dt, gc, hp, ch) = sems(
            nc, ctx, "b_weights_loaded", "b_fold_product", "b_fold_copied", "b_zeroed", "b_small_zeroed", "b_idx_ready",
            "b_transposed_in", "b_scanned", "b_transposed_back", "b_ends_built", "b_back_copied",
            "b_ends_picked", "b_picked_copied", "b_picked_turned", "b_windows_written", "b_features_split", "b_mlp_product", "b_relu_act",
            "b_relu_dve", "b_dots_done", "b_gates_copied", "b_high_parts", "b_chain")
        gat = sems(nc, ctx, *[f"b_gathered{q}" for q in range(NG)])
        ld = sems(nc, ctx, *[f"b_edge_data_loaded{q}" for q in range(NG)])
        gst = sems(nc, ctx, *[f"b_gates_stored{q}" for q in range(2)])
        wfr = ctx.enter_context(nc.sbuf_tensor("b_wf", [P, 2 * M * P], F32R))
        ear = [ctx.enter_context(nc.sbuf_tensor(f"b_ea{q}", [P, GJ * P], F32R)) for q in range(2)]
        ca = region(nc, ctx, "b_region", 11056)
        cb = Carve(t["acc"][:, 2:4, :].rearrange("p a b -> p (a b)"))
        G4 = GJ * P
        rows = ca(IJ * P).rearrange("p (s f) -> p s f", f=P)
        idx = ca(IJ, I32)
        rst = [ca(G4, BF16) for _ in range(NG)]
        w9 = [cb(G4, BF16) for _ in range(NG)]
        scan = [ca(G4) for _ in range(2)]
        back = [ca(G4) for _ in range(2)]
        picked = [ca(P) for _ in range(2)]
        ends = [ca(GJ * W) for _ in range(NG)]
        ends16 = [ca(GJ * W, BF16) for _ in range(NG)]
        ea = [cb(G4) for _ in range(NG)]
        rt = [[ca(G4) for _ in range(M)] for _ in range(2)]
        gout = [cb(G4) for _ in range(2)]
        bf, b1, w2 = ca(M), ca(M), ca(M)
        w2m = ca(M * W)
        ww9 = cb(P, BF16)
        ones16 = cb(P, BF16)
        weT, w1, be = cb(2 * DE, parts=DE), cb(M * P, parts=DE), cb(1, parts=DE)
        start, nil = cb(16), cb(1)
        bank = t["psum"]
        p1b, p2b, p3b, tb, gb = bank[0:2], bank[2], bank[3], bank[4:7], bank[7]
        ident, ones = t["ident"], t["ones"]
        P3 = [p3b[:, h * 256:h * 256 + 256].rearrange("p (a j w) -> p a j w", a=2, j=GJ) for h in range(2)]
        block = ctx.enter_context(nc.Block())
        CREDIT = NG

        @block.gpsimd
        def _(pool):
            for n, (s, per) in enumerate([(scd, 1), (p1, 1), (t2, 1), (ex, 1), (st, 1), (acd, GJ), (rd, 1), (dt, 1),
                                          (ra, 2), (tm, M), (gc, 1), (es, 1), (gst[0], 4), (gst[1], 4),
                                          (pk, 1), (pkc, 1)]):
                nc.gpsimd.memset(start[:, n:n + 1], 0.0).then_inc(s, per * CREDIT)
            gather_rows(nc, pool, t, d["B"], idx, rows, idxr, [(p1, 1)], gat, ahead=True)

        @block.sync
        def _(sp):
            sp.dma_start(weT[:, 0:DE], i["weT"]).then_inc(wld, 16)
            sp.dma_start(weT[:, DE:2 * DE], i["weT"]).then_inc(wld, 16)
            sp.dma_start(w1.rearrange("d (m f) -> d m f", m=M), i["w1"].rearrange("m d f -> d m f")).then_inc(wld, 16)
            sp.dma_start(be, i["be"]).then_inc(wld, 16)
            sp.dma_start(b1, i["b1T"]).then_inc(wld, 16)
            sp.dma_start(w2, i["w2T"]).then_inc(wld, 16)
            sp.wait_ge(zero9, 1)
            sp.dma_start(ww9[0:9, :], d["ww9"]).then_inc(wld, 16)
            nit = iterations(sp, t)

            def load(it, q):
                s = q % NG
                at = (it * NG + q) * G4
                sp.wait_ge(scd, it * NG + (q + 1))
                hold(sp)
                sp.dma_start(rst[s], d["reset"][bass.ds(at, G4)].partition_broadcast(P)).then_inc(ld[s], 16)
                sp.wait_ge(p1, it * NG + (q + 1))
                hold(sp)
                sp.dma_start(w9[s][0:9, :], d["w3"][:, bass.ds(at, G4)].unsqueeze(0).to_broadcast([3, 3, G4])
                             ).then_inc(ld[s], 16)
                sp.wait_ge(es, it * NG + (q + 1))
                hold(sp)
                for half in range(2):
                    sp.dma_start(ea[s][half * DE:(half + 1) * DE, :],
                                 i["eaT"][bass.ds(it * NG + q, 1), :, :].rearrange("a d e -> (a d) e")
                                 ).then_inc(ld[s], 16)

            load(0, 0)
            load(0, 1)
            load(0, 2)
            with sp.Fori(0, nit) as it:
                for q in range(NG):
                    load(it, q + 3)
                    sp.wait_ge(gc, it * NG + (q + 1 + CREDIT))
                    hold(sp)
                    store_gates(sp, d, gout[q % 2], it * NG + q, gst[q % 2])
            sp.wait_ge(wld, 7 * 16)
            for s in range(3):
                sp.wait_ge(ld[s], nit * 64 + 64)
                hold(sp)
            hold(sp)
            for n in range(2):
                sp.wait_ge(gst[n], nit * 32 + 16)
            hold(sp)

        @block.tensor
        def _(pe):
            pe.wait_ge(wld, 7 * 16)
            nc.tensor.matmul(bank[0][:, 0:M * P], weT, w1, start=True, stop=True)
            for m in range(M):
                last = nc.tensor.matmul(bank[1][:, m:m + 1], w1[:, m * P:(m + 1) * P], be, start=True, stop=True)
            last.then_inc(pre, 1)
            pe.wait_ge(pre2, 1)
            nit = iterations(pe, t)

            def rows_in(it, q):
                s = q % NG
                pe.wait_ge(gat[s], it * 64 + 64 * (q // NG + 1))
                pe.wait_ge(ld[s], it * 64 + 64 * (q // NG + 1))
                pe.wait_ge(scd, it * NG + (q - 2 + 1 + CREDIT))
                pe.wait_ge(pkc, it * NG + (q - 2 + 1 + CREDIT))
                b = p1b[q % 2]
                nc.tensor.matmul(b[:, :], ww9, w9[s], start=True, stop=False)
                for j in range(GJ):
                    last = nc.tensor.matmul(b[:, j * P:(j + 1) * P], rows[:, s * GJ + j, :], ident[:, :],
                                            start=False, stop=(j == GJ - 1))
                last.then_inc(p1, 1)

            def mlp(it, q):
                pe.wait_ge(es, it * NG + (q + 1 + CREDIT))
                for m in range(M):
                    if m < 2:
                        pe.wait_ge(ra, it * (2 * NG) + (2 * (q - 1 + CREDIT) + m + 1))
                    else:
                        pe.wait_ge(rd, it * NG + (q + CREDIT))
                    nc.tensor.matmul(tb[m][:, :], wfr[:, m * P:(m + 1) * P], ear[q % 2][:, :], start=True, stop=False)
                    nc.tensor.matmul(tb[m][:, :], wfr[:, (M + m) * P:(M + m + 1) * P], ear[q % 2][:, :],
                                     start=False, stop=True).then_inc(tm, 1)

            def rows_back(it, q):
                pe.wait_ge(scd, it * NG + (q + 1 + CREDIT))
                pe.wait_ge(st, it * NG + (q + CREDIT))
                for j in range(GJ):
                    last = nc.tensor.transpose(p2b[:, j * P:(j + 1) * P], scan[q % 2][:, j * P:(j + 1) * P],
                                               ident[:, :])
                last.then_inc(t2, 1)

            def dots(it, q):
                pe.wait_ge(ra, it * (2 * NG) + 2 * (q + 1 + CREDIT))
                pe.wait_ge(rd, it * NG + (q + 1 + CREDIT))
                pe.wait_ge(gc, it * NG + (q + CREDIT))
                for m in range(M):
                    last = nc.tensor.matmul(gb[m * W:(m + 1) * W, :], w2m[:, m * W:(m + 1) * W], rt[q % 2][m],
                                            start=True, stop=True)
                last.then_inc(dt, 1)

            def pick(it, q):
                pe.wait_ge(st, it * NG + (q + 1 + CREDIT))
                pe.wait_ge(ehd, it * (2 * NG) + 2 * (q + 1))
                for j in range(GJ):
                    last = nc.tensor.matmul(p1b[q % 2][j * W:(j + 1) * W, 0:P],
                                            ends[q][:, j * W:(j + 1) * W], back[q % 2][:, j * P:(j + 1) * P],
                                            start=True, stop=True)
                last.then_inc(pk, 1)

            def turn(it, q):
                pe.wait_ge(pkc, it * NG + (q + 1 + CREDIT))
                pe.wait_ge(acd, it * (NG * GJ) + (q - 1 + 1 + CREDIT) * GJ)
                nc.tensor.transpose(P3[q % 2][:, 0, :, :].rearrange("p j w -> p (j w)"), picked[q % 2], ident[:, :])
                nc.tensor.matmul(P3[q % 2][:, 1, :, :].rearrange("p j w -> p (j w)"), ones16, ends16[q],
                                 start=True, stop=True).then_inc(ex, 1)

            rows_in(0, 0)
            mlp(0, 0)
            rows_back(0, 0)
            with pe.Fori(0, nit) as it:
                for q in range(NG):
                    rows_in(it, q + 1)
                    pick(it, q)
                    mlp(it, q + 1)
                    dots(it, q)
                    rows_back(it, q + 1)
                    turn(it, q)

        @block.scalar
        def _(act):
            nit = iterations(act, t)
            act.wait_ge(zero, 1)
            nc.scalar.activation(t["acc"][:, 0, :], nil.to_broadcast([P, ACCW]), ACT.Copy).then_inc(zero, 1)
            act.wait_ge(zero, 3)

            def relus(it, q):
                for m in range(2):
                    act.wait_ge(tm, it * (3 * NG) + (3 * (q + CREDIT) + m + 1))
                    if m == 0:
                        act.wait_ge(dt, it * NG + (q - 2 + 1 + CREDIT))
                    nc.scalar.activation(rt[q % 2][m], tb[m][:, :], ACT.Relu, bias=bf[:, m:m + 1]).then_inc(ra, 1)

            def copy_back(it, q):
                act.wait_ge(t2, it * NG + (q + 1 + CREDIT))
                act.wait_ge(pk, it * NG + (q - 2 + 1 + CREDIT))
                nc.scalar.activation(back[q % 2], p2b[:, :], ACT.Copy).then_inc(st, 1)

            relus(0, 0)
            copy_back(0, 0)
            with act.Fori(0, nit) as it:
                for q in range(NG):
                    base = group_bases(nc, t, mybir.EngineType.Activation, it, q)
                    act.wait_ge(pk, it * NG + (q + 1 + CREDIT))
                    act.wait_ge(ex, it * NG + (q - 2 + 1 + CREDIT))
                    nc.scalar.activation(picked[q % 2], p1b[q % 2][:, 0:P], ACT.Copy).then_inc(pkc, 1)
                    relus(it, q + 1)
                    copy_back(it, q + 1)
                    act.wait_ge(ex, it * NG + (q + 1 + CREDIT))
                    for j in range(GJ):
                        act.wait_ge(acd, it * (NG * GJ) + ((q + CREDIT) * GJ + j))
                        nc.scalar.activation(t["acc"][:, 0:2, bass.ds(base[j], W)], P3[q % 2][:, :, j, :],
                                             ACT.Copy).then_inc(acd, 1)

        @block.vector
        def _(dve):
            c = Count(dve, ch)
            c.add(nc.vector.memset(scan[(NG - 1) % 2], -BIG))
            nc.vector.tensor_copy(idx, t["src_col"][:, 0:IJ]).then_inc(idxr, NG)
            nc.vector.memset(nil, 0.0).then_inc(zero, 1)
            c.add(nc.vector.memset(ww9, 0.0))
            c.add(nc.vector.memset(ones16, 1.0))
            c.add(nc.vector.memset(w2m, 0.0))
            for q in range(NG - 1):
                c.add(nc.vector.memset(w9[q], 0.0))
            c.wait()
            nc.vector.memset(w9[NG - 1], 0.0).then_inc(zero9, 1)
            nc.vector.memset(t["acc"][:, 1, :], 0.0).then_inc(zero, 1)
            dve.wait_ge(pre, 1)
            c.link(nc.vector.tensor_copy(wfr[:, 0:M * P], bank[0][:, 0:M * P]))
            c.add(nc.vector.tensor_copy(w2m.rearrange("p (m w) -> p m w", m=M)[:, :, 0], w2))
            c.link(nc.vector.tensor_tensor(wfr[:, M * P:2 * M * P], bank[0][:, 0:M * P],
                                           wfr[:, 0:M * P].bitcast(F32), ALU.subtract))
            nc.vector.tensor_tensor(bf, bank[1][:, 0:M], b1, ALU.add).then_inc(pre2, 1)
            c.wait()
            nit = iterations(dve, t)
            iota = t["iota_w"][:, :, :]

            def split_features(it, q):
                s, again, g = q % NG, q // NG, it * NG
                dve.wait_ge(ld[s], it * 64 + 64 * (again + 1))
                dve.wait_ge(tm, it * (3 * NG) + 3 * (q - 2 + 1 + CREDIT))
                nc.vector.tensor_copy(ear[q % 2][:, :], ea[s]).then_inc(hp, 1)
                dve.wait_ge(hp, g + (q + 1))
                nc.vector.tensor_tensor(ear[q % 2][DE:P, :], ea[s][DE:P, :], ear[q % 2][DE:P, :].bitcast(F32),
                                        ALU.subtract).then_inc(es, 1)

            def ahead(it, q):
                s, again, g = q % NG, q // NG, it * NG
                col = it * IJ + q * GJ
                dve.wait_ge(ld[s], it * 64 + 64 * (again + 1))
                dve.wait_ge(p1, g + (q + 1 + CREDIT))
                dve.wait_ge(t2, g + (q - 2 + 1 + CREDIT))
                dve.wait_ge(scd, g + (q + CREDIT))
                nc.vector.tensor_tensor_scan(scan[q % 2], rst[s], p1b[q % 2][:, :],
                                             scan[(q + 1) % 2][:, G4 - 1:G4], ALU.add, ALU.max).then_inc(scd, 1)
                split_features(it, q + 1)
                dve.wait_ge(ex, g + (q + 1))
                rel = t["end_col"][:, bass.ds(col, GJ)].unsqueeze(2).to_broadcast([P, GJ, W])
                nc.vector.tensor_tensor(ends[s].rearrange("p (j w) -> p j w", j=GJ), iota, rel,
                                        ALU.is_equal).then_inc(ehd, 1)
                nc.vector.tensor_tensor(ends16[s].rearrange("p (j w) -> p j w", j=GJ), iota, rel,
                                        ALU.is_equal).then_inc(ehd, 1)
                dve.wait_ge(gat[s], it * 64 + 64 * (again + 1))
                hold(dve)
                nc.vector.tensor_copy(idx[:, s * GJ:(s + 1) * GJ],
                                      t["src_col"][:, bass.ds(col + IJ, GJ)]).then_inc(idxr, 1)
                dve.wait_ge(tm, it * (3 * NG) + 3 * (q + 1 + CREDIT))
                dve.wait_ge(dt, g + (q - 2 + 1 + CREDIT))
                nc.vector.tensor_scalar(rt[q % 2][2], tb[2][:, :], bf[:, 2:3], 0.0, ALU.add,
                                        ALU.max).then_inc(rd, 1)

            split_features(0, 0)
            ahead(0, 0)
            with dve.Fori(0, nit) as it:
                for q in range(NG):
                    ahead(it, q + 1)
                    dve.wait_ge(dt, it * NG + (q + 1 + CREDIT))
                    dve.wait_ge(gst[q % 2], it * 32 + (16 * (q // 2) + 16))
                    nc.vector.tensor_copy(gout[q % 2][0:M * W, :], gb[0:M * W, :]).then_inc(gc, 1)


def hold(eng):
    eng.nop(nofuse=True)


def store_gates(sp, d, src, g, sem):
    sp.dma_start(d["gates"][bass.ds(g * GJ, GJ), :].rearrange("t (m e) -> m t e", m=M),
                 src[0:M * W:W, :].rearrange("m (t e) -> m t e", t=GJ)).then_inc(sem, 16)


def phase_softmax(nc, t, i, d, gates):
    heads = M if gates else 1
    with ExitStack() as ctx:
        (ld, first, sg, fs, cl, req, giv, xr, xd, done, ws, wl, tr2, tr2c, ch) = sems(
            nc, ctx, *[("c_" if gates else "e_") + n for n in (
                "loaded", "gathered" if gates else "transposed", "sigmoid", "flat_stored",
                "chunks_loaded", "carry_asked", "carry_given", "x_loaded" if gates else "exp_asked", "exp_done", "head_done",
                "weights_stored",
                "weights_loaded", "back_transposed", "back_copied", "chain")])
        gat = tr = first
        xl = xr
        ca = region(nc, ctx, "c_region" if gates else "e_region", 11400)
        valid, keep, stop = ca(FLAT), ca(FLAT), ca(FLAT)
        never, reset, go = ca(FLAT), ca(FLAT), ca(FLAT)
        v, f, b, e = ca(FLAT), ca(FLAT), ca(FLAT), ca(FLAT)
        mins = ca(3)
        minrow = [ca(P, parts=1) for _ in range(3)]
        row = ca(P, parts=1)
        crow = ca(P + 1, parts=1)
        ccol = ca(1)
        b2 = ca(M)
        entries = [v, never, reset] if gates else [v]
        weights = entries if gates else [e]
        if gates:
            cb = Carve(t["acc"][:, 2:4, :].rearrange("p a b -> p (a b)"))
            jg = cb(JC * M * P).rearrange("p (c m e) -> p c m e", c=JC, m=M)
            out = [cb(FLAT) for _ in range(M)]
            rows = [jg[:, :, m, :] for m in range(M)]
        else:
            rows = [v.rearrange("p (c e) -> p c e", e=P)]
            out = [v]
        bank = t["psum"]
        ident, ones = t["ident"], t["ones"]
        jrow = lambda ap: ap.rearrange("(c p e) -> p c e", p=P, e=P)
        chunk = lambda ap: ap.rearrange("(p n) -> p n", p=P)
        fwd, bwd = (f[:, FLAT - 1:FLAT], 0), (b[:, 0:1], 1)
        block = ctx.enter_context(nc.Block())

        @block.gpsimd
        def _(pool):
            if gates:
                for k in range(JC):
                    pool.indirect_dma_start(jg[:, k, :, :].rearrange("p m e -> p (m e)"), None,
                                            d["gates"][0:TC * P, :],
                                            bass.IndirectOffsetOnAxis(t["tile_of_job"][:, k:k + 1], 0)
                                            ).then_inc(gat, 16)

        @block.sync
        def _(sp):
            sp.dma_start(valid, chunk(d["valid"])).then_inc(ld, 16)
            sp.dma_start(keep, chunk(d["keep"])).then_inc(ld, 16)
            sp.dma_start(stop, chunk(d["stop"])).then_inc(ld, 16)
            if gates:
                sp.dma_start(b2, i["b2"].partition_broadcast(P)).then_inc(ld, 16)
            for m in range(heads):
                sp.wait_ge(sg, m + 1)
                sp.dma_start(jrow(d["flat"][m, :]), rows[m]).then_inc(fs, 16)
            sp.wait_ge(fs, 16 * heads)
            for m in range(heads):
                sp.dma_start(entries[m], chunk(d["flat"][m, :])).then_inc(cl, 16)
            if gates:
                sp.wait_ge(cl, 16 * heads)
                sp.dma_start(t["hT"][:, 0:NP], i["xT"]).then_inc(xl, 16)
            for m in range(heads):
                sp.wait_ge(done, m + 1)
                sp.dma_start(chunk(d["wflat"][m, :]), weights[m]).then_inc(ws, 16)
            sp.wait_ge(ws, 16 * heads)
            for m in range(heads):
                sp.dma_start(out[m].rearrange("p (c e) -> p c e", e=P), jrow(d["wflat"][m, :])).then_inc(wl, 16)
            if gates:
                sp.wait_ge(xl, 16)

        @block.scalar
        def _(act):
            if gates:
                act.wait_ge(gat, 16 * JC)
                act.wait_ge(ld, 64)
                for m in range(M):
                    nc.scalar.activation(rows[m], rows[m], ACT.Sigmoid, bias=b2[:, m:m + 1]).then_inc(sg, 1)
            for m in range(heads):
                if gates:
                    act.wait_ge(cl, 16 * heads)
                    nc.scalar.activation(weights[m], entries[m], ACT.Exp).then_inc(xd, 1)
                else:
                    act.wait_ge(xr, 1)
                    nc.scalar.activation(weights[0], weights[0], ACT.Exp).then_inc(xd, 1)

        @block.tensor
        def _(pe):
            if not gates:
                for k in range(JC):
                    last = nc.tensor.transpose(bank[2 + k // 4][:, k % 4 * P:k % 4 * P + P],
                                               t["att_col"][:, k * P:(k + 1) * P], ident[:, :])
                last.then_inc(tr, 1)
            n = 0
            for k in (1, 2) if gates else (0, 1, 2):
                n += 1
                pe.wait_ge(req, n)
                nc.tensor.matmul(bank[0][0:1, 0:P], mins[:, k:k + 1], ident[:, :], start=True, stop=True
                                 ).then_inc(giv, 1)
            for m in range(heads):
                for last_state, off in (fwd, bwd) if gates else (fwd, bwd, fwd, bwd):
                    n += 1
                    pe.wait_ge(req, n)
                    nc.tensor.matmul(bank[0][0:1, 0:P], last_state, ident[:, :], start=True, stop=True
                                     ).then_inc(giv, 1)
                    n += 1
                    pe.wait_ge(req, n)
                    nc.tensor.matmul(bank[1][:, 0:1], crow[:, off:off + P], ones[0:1, 0:1], start=True, stop=True
                                     ).then_inc(giv, 1)
            pe.wait_ge(wl, 16 * heads)
            for m in range(heads):
                for half in range(2):
                    if m:
                        pe.wait_ge(tr2c, 2 * m - 1 + half)
                    for k in range(4):
                        last = nc.tensor.transpose(bank[2 + half][:, k * P:(k + 1) * P],
                                                   out[m][:, (half * 4 + k) * P:(half * 4 + k + 1) * P], ident[:, :])
                    last.then_inc(tr2, 1)

        @block.vector
        def _(dve):
            c = Count(dve, ch)
            asked = [0]

            def ask(ins):
                asked[0] += 1
                ins.then_inc(req, 1)
                dve.wait_ge(giv, asked[0])

            if not gates:
                dve.wait_ge(tr, 1)
                c.add(nc.vector.tensor_copy(v[:, 0:512], bank[2][:, :]))
                nc.vector.tensor_copy(v[:, 512:FLAT], bank[3][:, :]).then_inc(sg, 1)
                c.wait()
            dve.wait_ge(ld, 64 if gates else 48)
            if not gates:
                c.add(nc.vector.tensor_scalar(never, valid, 1.0, BIG, ALU.subtract, ALU.mult))
                c.add(nc.vector.tensor_scalar(reset, keep, 1.0, BIG, ALU.subtract, ALU.mult))
            c.link(nc.vector.tensor_scalar(go, stop, -1.0, 1.0, ALU.mult, ALU.add))
            for k, src in ((1, keep), (2, go)) if gates else ((0, reset), (1, keep), (2, go)):
                ask(nc.vector.tensor_reduce(mins[:, k:k + 1], src, X, ALU.min))
                c.link(nc.vector.tensor_copy(minrow[k], bank[0][0:1, 0:P]))

            def carried(last, through, op0, op1, init, back):
                c.wait()
                ask(nc.vector.memset(crow, init))
                c.link(nc.vector.tensor_copy(row, bank[0][0:1, 0:P]))
                if back:
                    ask(nc.vector.tensor_tensor_scan(crow[:, 0:P][:, ::-1], through[:, ::-1], row[:, ::-1], init,
                                                     op0, op1))
                else:
                    ask(nc.vector.tensor_tensor_scan(crow[:, 1:P + 1], through, row, init, op0, op1))
                c.link(nc.vector.tensor_copy(ccol, bank[1][:, 0:1]))

            def over(out_, keep_, x, minrow_, op0, op1, init):
                c.link(nc.vector.tensor_tensor_scan(out_, keep_, x, init, op0, op1))
                carried(out_, minrow_, op0, op1, init, False)
                c.link(nc.vector.tensor_tensor_scan(out_, keep_, x, ccol, op0, op1))

            def handed_back():
                c.link(nc.vector.tensor_tensor(f, f, stop, ALU.mult))
                c.link(nc.vector.tensor_tensor_scan(b[:, ::-1], go[:, ::-1], f[:, ::-1], 0.0, ALU.mult, ALU.add))
                carried(b, minrow[2], ALU.mult, ALU.add, 0.0, True)
                c.link(nc.vector.tensor_tensor_scan(b[:, ::-1], go[:, ::-1], f[:, ::-1], ccol, ALU.mult, ALU.add))

            for m in range(heads):
                if not gates:
                    dve.wait_ge(cl, 16)
                    c.link(nc.vector.tensor_tensor(v, v, never, ALU.add))
                    over(f, reset, v, minrow[0], ALU.add, ALU.max, -BIG)
                    handed_back()
                    nc.vector.tensor_tensor(weights[0], v, b, ALU.subtract).then_inc(xr, 1)
                e = weights[m]
                dve.wait_ge(xd, m + 1)
                c.link(nc.vector.tensor_tensor(e, e, valid, ALU.mult))
                over(f, keep, e, minrow[1], ALU.mult, ALU.add, 0.0)
                handed_back()
                c.link(nc.vector.tensor_scalar(b, b, 0.5, None, ALU.max))
                c.link(nc.vector.reciprocal(b, b))
                nc.vector.tensor_tensor(e, e, b, ALU.mult).then_inc(done, 1)
            for m in range(heads):
                for half in range(2):
                    dve.wait_ge(tr2, 2 * m + half + 1)
                    dst = t["gate_col"][:, m, :] if gates else t["att_col"][:, :]
                    nc.vector.tensor_copy(dst[:, half * 512:half * 512 + 512], bank[2 + half][:, :]).then_inc(tr2c, 1)


def layer_norm(c, act_ask, act_done, n, parts, mean, cen, sq, std, out, before_out=()):
    v = c.eng
    for (a, z), view in parts:
        c.add(v.reduce_sum(mean[:, a:z], view, X))
    c.wait()
    c.link(v.tensor_scalar(mean, mean, 1.0 / D, None, ALU.mult))
    for (a, z), view in parts:
        c.add(v.tensor_tensor(cen[:, a:z, :], view, mean[:, a:z].unsqueeze(2).to_broadcast([P, z - a, D]),
                              ALU.subtract))
    c.wait()
    c.link(v.tensor_tensor(sq, cen, cen, ALU.mult))
    v.reduce_sum(std, sq, X).then_inc(act_ask, 1)
    v.wait_ge(act_done, n)
    c.link(v.reciprocal(std, std))
    for sem, value in before_out:
        v.wait_ge(sem, value)
    return v.tensor_tensor(out, cen, std.unsqueeze(2).to_broadcast([P, CB, D]), ALU.mult)


HALVES = [(0, 4), (4, CB)]


def blocks_view(bank, a, z):
    return bank[:, 0:(z - a) * P].rearrange("p (b f) -> p b f", f=P)


def phase_nodes0(nc, t, i, d):
    with ExitStack() as ctx:
        (wld, xrl, xb, xu, sA, sF, hsc, sH, sR, sO, ask, root, ln, sT, sTc, shl, sh, shc, x1s, hst, eps_s, ch, chn) = sems(
            nc, ctx, *["n_" + n for n in (
                "weights_loaded", "x_rows_loaded", "x_rows_biased", "x_rows_used", "dst_part", "agg_full",
                "has_copied", "hidden", "relu", "out", "root_asked",
                "root_done", "normed", "x1_transposed", "x1_copied", "h_columns", "h_rows", "h_copied",
                "x1_stored", "h_stored", "eps", "chain", "norm_chain")])
        ca = region(nc, ctx, "n_region", 12600)
        cb = Carve(t["acc"][:, 2:4, :].rearrange("p a b -> p (a b)"))
        wd, w1a, w1b, w2, fc = (ca(P) for _ in range(5))
        bm, b1, fcb, gw, eps = (ca(1) for _ in range(5))
        b2r, fcbr = ca(P), ca(P, parts=1)
        agg, hid, x1T, hasc = (ca(CN) for _ in range(4))
        xT = t["hT"]
        d3 = lambda: cb(CN).rearrange("p (b f) -> p b f", f=P)
        cen, sq, x1, hrow = d3(), d3(), d3(), d3()
        xrow, v = (ca(CN).rearrange("p (b f) -> p b f", f=P) for _ in range(2))
        mean, std = ca(CB), ca(CB)
        start = ca(4)
        bank = t["psum"]
        ident, ones = t["ident"], t["ones"]
        acc = t["acc"]
        H = CN // 2
        SIDE = (CB - 4) * P
        block = ctx.enter_context(nc.Block())

        @block.sync
        def _(sp):
            for dst, src in ((wd, i["Wm"][0:D, :]), (w1a, i["W1"][0:D, :]), (w1b, i["W1"][D:2 * D, :]), (w2, i["W2"]),
                             (fc, i["fc"]), (bm, i["bm"]), (b1, i["b1"]), (fcb, i["fcb"]), (gw, i["gw"]),
                             (b2r, i["b2v"].partition_broadcast(P)), (fcbr, i["fcbrow"])):
                sp.dma_start(dst, src).then_inc(wld, 16)
            sp.dma_start(xrow, i["xrow"][0:CN, :].rearrange("(b p) f -> p b f", p=P)).then_inc(xrl, 16)
            with sp.Fori(0, NCH) as c:
                sp.wait_ge(xu, c + 1)
                hold(sp)
                sp.dma_start(xrow, i["xrow"][bass.ds(c * CN + CN, CN), :].rearrange("(b p) f -> p b f", p=P)
                             ).then_inc(xrl, 16)
                sp.wait_ge(ln, c + 1)
                hold(sp)
                sp.dma_start(d["x1"][bass.ds(c * CN, CN), :].rearrange("(b p) f -> p b f", p=P), x1).then_inc(x1s, 16)
                sp.wait_ge(shc, c * 4 + 8)
                hold(sp)
                sp.dma_start(d["h"][bass.ds(c * CN, CN), :].rearrange("(b p) f -> p b f", p=P), hrow).then_inc(hst, 16)
            sp.wait_ge(xrl, 16 * NCH + 16)
            sp.wait_ge(x1s, 16 * NCH + 16)
            sp.wait_ge(hst, 16 * NCH + 16)

        @block.gpsimd
        def _(pool):
            for n, (s, per) in enumerate([(hst, 16), (x1s, 16), (shc, 4)]):
                nc.gpsimd.memset(start[:, n:n + 1], 0.0).then_inc(s, per)
            pool.wait_ge(wld, 11 * 16)
            with pool.Fori(0, NCH) as c:
                pool.wait_ge(xrl, c * 16 + 16)
                nc.gpsimd.tensor_tensor(xrow, xrow, b2r.unsqueeze(1).to_broadcast([P, CB, P]), ALU.add).then_inc(xb, 1)

        @block.tensor
        def _(pe):
            pe.wait_ge(wld, 11 * 16)

            def x(c, h):
                return xT[:, bass.ds(c * CN + h * H, H)]

            def of_dst(c):
                pe.wait_ge(sF, c)
                for h in range(2):
                    last = nc.tensor.matmul(bank[h][:, 0:H], wd, x(c, h), start=True, stop=True)
                last.then_inc(sA, 1)

            def hidden(c):
                pe.wait_ge(sF, c + 1)
                for h in range(2):
                    nc.tensor.matmul(bank[2 + h][:, 0:H], w1a, x(c, h), start=True, stop=False)
                    last = nc.tensor.matmul(bank[2 + h][:, 0:H], w1b, agg[:, h * H:(h + 1) * H], start=False, stop=True)
                last.then_inc(sH, 1)

            def out(c):
                pe.wait_ge(sR, c + 1)
                pe.wait_ge(xu, c)
                pe.wait_ge(hsc, c + 1)
                for h, (a, z) in enumerate(HALVES):
                    for k in range(a, z):
                        nc.tensor.matmul(bank[4 + h][:, (k - a) * P:(k - a + 1) * P], hid[:, k * P:(k + 1) * P], w2,
                                         start=True, stop=True)
                for k in range(CB):
                    last = nc.tensor.matmul(bank[5][:, SIDE + k:SIDE + k + 1], hasc[:, k * P:(k + 1) * P],
                                            ident[:, 0:1], start=True, stop=True)
                last.then_inc(sO, 1)

            def turn(c):
                pe.wait_ge(ln, c + 1)
                pe.wait_ge(shc, c * 4 + 4)
                for h, (a, z) in enumerate(HALVES):
                    for k in range(a, z):
                        last = nc.tensor.transpose(bank[6 + h][:, (k - a) * P:(k - a + 1) * P], x1[:, k, :], ident[:, :])
                last.then_inc(sT, 1)

            def h_of(c):
                pe.wait_ge(sTc, c + 1)
                for h in range(2):
                    last = nc.tensor.matmul(bank[2 + h][:, 0:H], fc, x1T[:, h * H:(h + 1) * H], start=True, stop=True)
                last.then_inc(shl, 1)
                for h, (a, z) in enumerate(HALVES):
                    for k in range(a, z):
                        o = bank[6 + h][:, (k - a) * P:(k - a + 1) * P]
                        nc.tensor.matmul(o, x1T[:, k * P:(k + 1) * P], fc, start=True, stop=False)
                        nc.tensor.matmul(o, ones[0:1, :], fcbr, start=False, stop=True)
                for k in range(CB):
                    last = nc.tensor.matmul(bank[7][:, SIDE + k:SIDE + k + 1], x1T[:, k * P:(k + 1) * P], gw,
                                            start=True, stop=True)
                last.then_inc(sh, 1)

            of_dst(0)
            hidden(0)
            of_dst(1)
            out(0)
            with pe.Fori(0, NCH - 2) as c:
                of_dst(c + 2)
                pe.wait_ge(shc, c * 4 + 2)
                hidden(c + 1)
                out(c + 1)
                turn(c)
                h_of(c)
            pe.wait_ge(shc, (NCH - 2) * 4 + 2)
            hidden(NCH - 1)
            out(NCH - 1)
            turn(NCH - 2)
            h_of(NCH - 2)
            turn(NCH - 1)
            h_of(NCH - 1)

        @block.scalar
        def _(act):
            act.wait_ge(wld, 11 * 16)
            act.wait_ge(eps_s, 2)

            def relu(c):
                act.wait_ge(sH, c + 1)
                nc.scalar.activation(hid[:, 0:H], bank[2][:, 0:H], ACT.Relu, bias=b1)
                nc.scalar.activation(hid[:, H:CN], bank[3][:, 0:H], ACT.Relu, bias=b1).then_inc(sR, 1)

            def square_root(c):
                act.wait_ge(ask, c + 2)
                nc.scalar.activation(std, std, ACT.Sqrt, bias=eps, scale=1.0 / D).then_inc(root, 1)

            def copy_x1(c):
                act.wait_ge(sT, c + 1)
                for h, (a, z) in enumerate(HALVES):
                    last = nc.scalar.activation(x1T[:, a * P:z * P], bank[6 + h][:, 0:(z - a) * P], ACT.Copy)
                last.then_inc(sTc, 1)

            def copy_h(c):
                act.wait_ge(shl, c + 1)
                for h in range(2):
                    nc.scalar.activation(t["hT"][:, bass.ds(c * CN + h * H, H)], bank[2 + h][:, 0:H], ACT.Identity,
                                         bias=fcb).then_inc(shc, 1)
                act.wait_ge(sh, c + 1)
                act.wait_ge(hst, c * 16 + 16)
                hold(act)
                nc.scalar.activation(t["gate_n"][:, bass.ds(c * CB, CB)], bank[7][:, SIDE:SIDE + CB], ACT.Copy)
                for h, (a, z) in enumerate(HALVES):
                    nc.scalar.activation(hrow[:, a:z, :], blocks_view(bank[6 + h], a, z), ACT.Copy).then_inc(shc, 1)

            def copy_has(c):
                act.wait_ge(sO, c)
                hold(act)
                nc.scalar.activation(hasc, acc[:, 1, bass.ds(c * CN, CN)], ACT.Copy).then_inc(hsc, 1)

            copy_has(0)
            relu(0)
            square_root(0)
            with act.Fori(0, NCH - 1) as c:
                copy_has(c + 1)
                relu(c + 1)
                copy_x1(c)
                square_root(c + 1)
                copy_h(c)
            copy_x1(NCH - 1)
            copy_h(NCH - 1)

        @block.vector
        def _(dve):
            nc.vector.memset(eps, EPS).then_inc(eps_s, 1)
            nc.vector.memset(t["hT"][:, NP:ACCW], 0.0).then_inc(eps_s, 1)
            nc.vector.memset(mean, 0.0).then_inc(ask, 1)
            dve.wait_ge(wld, 11 * 16)
            PER, PERN = 2, 1 + 5

            def aggregate(it):
                c = Count(dve, ch, it * PER)
                dve.wait_ge(sA, it + 1)
                dve.wait_ge(sH, it)
                for h in range(2):
                    at = it * CN + h * H
                    c.add(nc.vector.scalar_tensor_tensor(agg[:, h * H:(h + 1) * H], bank[h][:, 0:H], bm,
                                                         acc[:, 1, bass.ds(at, H)], ALU.add, ALU.mult))
                c.wait()
                nc.vector.tensor_tensor(agg, agg, acc[:, 0, bass.ds(it * CN, CN)], ALU.add).then_inc(sF, 1)

            def norm(it):
                c = Count(dve, chn, it * PERN)
                dve.wait_ge(sO, it + 1)
                dve.wait_ge(xb, it + 1)
                hold(dve)
                c.add(nc.vector.tensor_copy(t["has_n"][:, bass.ds(it * CB, CB)], bank[5][:, SIDE:SIDE + CB]))
                for h, (a, z) in enumerate(HALVES):
                    last = nc.vector.tensor_tensor(v[:, a:z, :], blocks_view(bank[4 + h], a, z), xrow[:, a:z, :],
                                                   ALU.add)
                last.then_inc(xu, 1)
                dve.wait_ge(xu, it + 1)
                layer_norm(c, ask, root, it + 1, [((0, CB), v)], mean, cen, sq, std, x1,
                           before_out=[(x1s, it * 16 + 16), (sT, it)]).then_inc(ln, 1)
                assert c.n == PERN

            aggregate(0)
            aggregate(1)
            norm(0)
            with dve.Fori(0, NCH - 2) as c:
                aggregate(c + 2)
                norm(c + 1)
            norm(NCH - 1)


def one_hot(nc, t, table, col, out):
    rel = table[:, bass.ds(col, GJ)].unsqueeze(2).to_broadcast([P, GJ, W])
    return nc.vector.tensor_tensor(out, t["iota_w"][:, :, :], rel, ALU.is_equal)


def phase_scores(nc, t, i, d):
    with ExitStack() as ctx:
        (zero, idxr, tp, hc, wbr, wbs, gw, amd, acd, ohs, ats) = sems(nc, ctx, *["d_" + n for n in (
            "zeroed", "idx_ready", "transposed", "columns_copied", "weights_built", "sums_done",
            "products_done", "products_masked", "windows_added", "one_hot", "scores_stored")])
        gat = sems(nc, ctx, *[f"d_gathered{q}" for q in range(NG)])
        sst = sems(nc, ctx, *[f"d_rows_stored{q}" for q in range(NG)])
        ca = region(nc, ctx, "d_region", 9000)
        G4 = GJ * P
        rows = ca(IJ * P).rearrange("p (s f) -> p s f", f=P)
        idx = ca(IJ, I32)
        hs = [ca(G4) for _ in range(2)]
        oh = [ca(GJ * W).rearrange("p (j w) -> p j w", j=GJ) for _ in range(2)]
        wb = [ca(GJ * M * W).rearrange("p (j m w) -> p j m w", j=GJ, m=M) for _ in range(2)]
        am = [ca(GJ * W).rearrange("p (j w) -> p j w", j=GJ) for _ in range(2)]
        start = ca(16)
        bank = t["psum"]
        tb, sb, pb = bank[0:2], bank[2:4], bank[4:6]
        acc = t["acc"]
        block = ctx.enter_context(nc.Block())
        CREDIT = NG

        @block.gpsimd
        def _(pool):
            for n, (s, per) in enumerate([(tp, 1), (hc, 1), (wbr, 1), (wbs, 1), (gw, 1), (amd, 1), (acd, GJ), (ats, 1)] + [(s, 4) for s in sst]):
                nc.gpsimd.memset(start[:, n:n + 1], 0.0).then_inc(s, per * CREDIT)
            gather_rows(nc, pool, t, d["h"], idx, rows, idxr, [(tp, 1), (wbs, 1)], gat, sst)

        @block.sync
        def _(sp):
            nit = iterations(sp, t)
            with sp.Fori(0, nit) as it:
                for q in range(NG):
                    sp.wait_ge(gat[q], it * 64 + 64)
                    hold(sp)
                    sp.dma_start(d["hsp"][bass.ds(it * NG + q, 1), :, :].rearrange("a p n -> (a p) n"),
                                 rows[:, q * GJ:(q + 1) * GJ, :].rearrange("p s f -> p (s f)")).then_inc(sst[q], 16)
            for q in range(NG):
                sp.wait_ge(sst[q], nit * 16 + 16)
            hold(sp)

        @block.tensor
        def _(pe):
            nit = iterations(pe, t)
            with pe.Fori(0, nit) as it:
                for q in range(NG):
                    g = it * NG
                    base = group_bases(nc, t, mybir.EngineType.PE, it, q)
                    pe.wait_ge(gat[q], it * 64 + 64)
                    pe.wait_ge(hc, g + (q - 2 + 1 + CREDIT))
                    for j in range(GJ):
                        last = nc.tensor.transpose(tb[q % 2][:, j * P:(j + 1) * P], rows[:, q * GJ + j, :],
                                                   t["ident"][:, :])
                    last.then_inc(tp, 1)
                    pe.wait_ge(wbr, g + (q + 1 + CREDIT))
                    pe.wait_ge(acd, it * (NG * GJ) + (q - 2 + 1 + CREDIT) * GJ)
                    for j in range(GJ):
                        last = nc.tensor.matmul(sb[q % 2][:, j * M * W:(j + 1) * M * W], rows[:, q * GJ + j, :],
                                                wb[q % 2][:, j, :, :].rearrange("p m w -> p (m w)"),
                                                start=True, stop=True)
                    last.then_inc(wbs, 1)
                    pe.wait_ge(hc, g + (q + 1 + CREDIT))
                    pe.wait_ge(amd, g + (q - 2 + 1 + CREDIT))
                    for j in range(GJ):
                        last = nc.tensor.matmul(pb[q % 2][:, j * W:(j + 1) * W], hs[q % 2][:, j * P:(j + 1) * P],
                                                t["hT"][:, bass.ds(base[j], W)], start=True, stop=True)
                    last.then_inc(gw, 1)

        @block.scalar
        def _(act):
            act.wait_ge(zero, 1)
            for k in range(2, 1 + M):
                nc.scalar.activation(acc[:, k, :], t["att_col"][:, 0:1].to_broadcast([P, ACCW]), ACT.Copy
                                     ).then_inc(zero, 1)
            nit = iterations(act, t)
            with act.Fori(0, nit) as it:
                for q in range(NG):
                    act.wait_ge(tp, it * NG + (q + 1 + CREDIT))
                    act.wait_ge(gw, it * NG + (q - 2 + 1 + CREDIT))
                    nc.scalar.activation(hs[q % 2], tb[q % 2][:, :], ACT.Copy).then_inc(hc, 1)

        @block.vector
        def _(dve):
            nc.vector.tensor_copy(idx, t["src_col"][:, 0:IJ]).then_inc(idxr, NG)
            nc.vector.memset(t["att_col"][:, :], 0.0).then_inc(zero, 1)
            for k in range(2):
                nc.vector.memset(acc[:, k, :], 0.0).then_inc(zero, 1)
            dve.wait_ge(zero, 5)

            def weights(it, q):
                g = it * NG
                col = it * IJ + q * GJ
                dve.wait_ge(amd, g + (q - 2 + 1 + CREDIT))
                one_hot(nc, t, t["rel_col"], col, oh[q % 2]).then_inc(ohs, 1)
                dve.wait_ge(ohs, g + (q + 1))
                dve.wait_ge(wbs, g + (q - 2 + 1 + CREDIT))
                nc.vector.tensor_tensor(
                    wb[q % 2], oh[q % 2].unsqueeze(2).to_broadcast([P, GJ, M, W]),
                    t["gate_col"][:, :, bass.ds(col, GJ)].rearrange("p m j -> p j m").unsqueeze(3)
                    .to_broadcast([P, GJ, M, W]), ALU.mult).then_inc(wbr, 1)

            weights(0, 0)
            nit = iterations(dve, t)
            with dve.Fori(0, nit) as it:
                for q in range(NG):
                    g = it * NG
                    col = it * IJ + q * GJ
                    base = group_bases(nc, t, mybir.EngineType.DVE, it, q)
                    weights(it, q + 1)
                    dve.wait_ge(gat[q], it * 64 + 64)
                    hold(dve)
                    nc.vector.tensor_copy(idx[:, q * GJ:(q + 1) * GJ],
                                          t["src_col"][:, bass.ds(col + IJ, GJ)]).then_inc(idxr, 1)
                    dve.wait_ge(wbs, g + (q + 1 + CREDIT))
                    for j in range(GJ):
                        dve.wait_ge(acd, it * (NG * GJ) + ((q + CREDIT) * GJ + j))
                        w = acc[:, 1:1 + M, bass.ds(base[j], W)]
                        nc.vector.tensor_tensor(w, w, sb[q % 2][:, j * M * W:(j + 1) * M * W].rearrange(
                            "p (m w) -> p m w", m=M), ALU.add).then_inc(acd, 1)
                    dve.wait_ge(gw, g + (q + 1 + CREDIT))
                    dve.wait_ge(ats, g + (q - 2 + 1 + CREDIT))
                    nc.vector.tensor_tensor(am[q % 2], pb[q % 2][:, 0:GJ * W].rearrange("p (j w) -> p j w", j=GJ),
                                            oh[q % 2], ALU.mult).then_inc(amd, 1)
                    dve.wait_ge(amd, g + (q + 1 + CREDIT))
                    nc.vector.reduce_sum(t["att_col"][:, bass.ds(col, GJ)], am[q % 2], X).then_inc(ats, 1)


def phase_sums(nc, t, i, d):
    with ExitStack() as ctx:
        (ohs, war, ws, wc, wt, wtc, acd, acp, zero) = sems(
            nc, ctx, "f_one_hot", "f_weights_built", "f_sums_done", "f_sums_copied", "f_sums_transposed",
            "f_turned_copied", "f_even_windows_added", "f_odd_windows_added", "f_zeroed")
        ld = sems(nc, ctx, *[f"f_rows_loaded{q}" for q in range(NG)])
        ca = region(nc, ctx, "f_region", 6000)
        G4 = GJ * P
        rows = [ca(G4) for _ in range(NG)]
        oh = [ca(GJ * W).rearrange("p (j w) -> p j w", j=GJ) for _ in range(NG)]
        wa = [ca(GJ * W).rearrange("p (j w) -> p j w", j=GJ) for _ in range(NG)]
        sums = [ca(P) for _ in range(2)]
        turned = [ca(P) for _ in range(2)]
        start = ca(16)
        bank = t["psum"]
        block = ctx.enter_context(nc.Block())
        HALF = GJ // 2

        def add_window(eng, into, it, q, bases, k, odd, added):
            j = 2 * k + odd
            eng.wait_ge(added, it * (NG * HALF) + ((q + CREDIT) * HALF + k))
            w = into[:, bass.ds(bases[q * GJ + j], W)]
            eng.tensor_tensor(w, w, turned[q % 2][:, j * W:(j + 1) * W], ALU.add).then_inc(added, 1)

        CREDIT = NG

        @block.sync
        def _(sp):
            nit = iterations(sp, t)
            with sp.Fori(0, nit) as it:
                for q in range(NG):
                    sp.wait_ge(ws, it * NG + (q + 1))
                    hold(sp)
                    sp.dma_start(rows[q], d["hsp"][bass.ds(it * NG + q, 1), :, :].rearrange("a p n -> (a p) n")
                                 ).then_inc(ld[q], 16)
            sp.wait_ge(ws, nit * NG + 1)
            hold(sp)
            sp.dma_start(rows[0], d["hsp"][0, :, :]).then_inc(ld[0], 16)

        @block.tensor
        def _(pe):
            nit = iterations(pe, t)

            def sum_rows(it, q):
                pe.wait_ge(ld[q % NG], it * 16 + 16 * (q // NG + 1))
                pe.wait_ge(war, it * NG + (q + 1 + CREDIT))
                pe.wait_ge(wc, it * NG + (q - 2 + 1 + CREDIT))
                for j in range(GJ):
                    last = nc.tensor.matmul(bank[q % 2][j * W:(j + 1) * W, 0:P], wa[q % NG][:, j, :],
                                            rows[q % NG][:, j * P:(j + 1) * P], start=True, stop=True)
                last.then_inc(ws, 1)

            sum_rows(0, 0)
            with pe.Fori(0, nit) as it:
                for q in range(NG):
                    g = it * NG
                    sum_rows(it, q + 1)
                    pe.wait_ge(wc, g + (q + 1 + CREDIT))
                    pe.wait_ge(wtc, g + (q - 2 + 1 + CREDIT))
                    nc.tensor.transpose(bank[2 + q % 2][:, 0:P], sums[q % 2], t["ident"][:, :]).then_inc(wt, 1)

        @block.scalar
        def _(act):
            nit = iterations(act, t)

            def copy_sums(it, q):
                act.wait_ge(ws, it * NG + (q + 1 + CREDIT))
                act.wait_ge(wt, it * NG + (q - 2 + 1 + CREDIT))
                nc.scalar.activation(sums[q % 2], bank[q % 2][:, 0:P], ACT.Copy).then_inc(wc, 1)

            copy_sums(0, 0)
            with act.Fori(0, nit) as it:
                for q in range(NG):
                    copy_sums(it, q + 1)
                    act.wait_ge(wt, it * NG + (q + 1 + CREDIT))
                    for added in (acd, acp):
                        act.wait_ge(added, it * (NG * HALF) + (q - 2 + 1 + CREDIT) * HALF)
                    nc.scalar.activation(turned[q % 2], bank[2 + q % 2][:, 0:P], ACT.Copy).then_inc(wtc, 1)

        @block.gpsimd
        def _(pool):
            for n, (s, per) in enumerate([(ohs, 1), (war, 1), (ws, 1), (wc, 1), (wt, 1), (wtc, 1), (acd, HALF),
                                          (acp, HALF)]):
                nc.gpsimd.memset(start[:, n:n + 1], 0.0).then_inc(s, per * CREDIT)
            nit = iterations(pool, t)
            pool.wait_ge(zero, 1)
            with pool.Fori(0, nit) as it:
                bases = iteration_bases(nc, t, mybir.EngineType.Pool, it)
                for q in range(NG):
                    pool.wait_ge(wtc, it * NG + (q + 1 + CREDIT))
                    for k in range(HALF):
                        add_window(nc.gpsimd, t["hT"], it, q, bases, k, 1, acp)

        @block.vector
        def _(dve):

            def hot(it, q):
                dve.wait_ge(war, it * NG + (q - NG + 1 + CREDIT))
                one_hot(nc, t, t["rel_col"], it * IJ + q * GJ, oh[q % NG]).then_inc(ohs, 1)

            def weights(it, q):
                dve.wait_ge(ohs, it * NG + (q + 1 + CREDIT))
                dve.wait_ge(ws, it * NG + (q - NG + 1 + CREDIT))
                nc.vector.tensor_tensor(
                    wa[q % NG], oh[q % NG],
                    t["att_col"][:, bass.ds(it * IJ + q * GJ, GJ)].unsqueeze(2).to_broadcast([P, GJ, W]),
                    ALU.mult).then_inc(war, 1)

            for q in range(NG):
                hot(0, q)
            for q in range(NG - 1):
                weights(0, q)
            nc.vector.memset(t["hT"][:, :], 0.0).then_inc(zero, 1)
            nit = iterations(dve, t)
            with dve.Fori(0, nit) as it:
                bases = iteration_bases(nc, t, mybir.EngineType.DVE, it)
                for q in range(NG):
                    hot(it, q + NG)
                    dve.wait_ge(wtc, it * NG + (q + 1 + CREDIT))
                    add_window(nc.vector, t["acc"][:, 0, :], it, q, bases, 0, 0, acd)
                    weights(it, q + 3)
                    add_window(nc.vector, t["acc"][:, 0, :], it, q, bases, 1, 0, acd)


def phase_nodes1(nc, t, i, d, out):
    with ExitStack() as ctx:
        (wld, wp, wc, gs, cf, sj, hl, xl, su, sr, sT, su_v, mx, mxc, ask, root, ln, ost, eps_s, ch) = sems(
            nc, ctx, *["g_" + n for n in (
                "weights_loaded", "weight_products", "weights_copied", "gate", "coefficients",
                "sums_joined", "h_loaded", "x1_loaded",
                "out_product", "relu", "transposed", "transposed_read", "rest_mixed", "rest_chain", "root_asked",
                "root_done", "normed", "stored", "eps", "chain")])
        ca = region(nc, ctx, "g_region", 12600)
        att, rel = ca(M * P), ca(M * P)
        o1, o2 = ca(P), ca(P)
        w = [ca(P) for _ in range(1 + M)]
        ob, gb, eps = ca(1), ca(1), ca(1)
        gate, cu, chh, cx = (ca(NBLK) for _ in range(4))
        u = ca(CN)
        c3 = lambda: ca(CN).rearrange("p (b f) -> p b f", f=P)
        h, x1, v, cen, sq, y = (c3() for _ in range(6))
        rest = [c3() for _ in range(1)][0]
        mean, std = ca(CB), ca(CB)
        start = ca(5)
        bank = t["psum"]
        ident = t["ident"]
        acc = t["acc"]
        H = CN // 2
        block = ctx.enter_context(nc.Block())

        @block.sync
        def _(sp):
            for dst, src in ((att.rearrange("p (m f) -> p m f", m=M), i["attT"].rearrange("m j d -> j m d")),
                             (rel.rearrange("p (m f) -> p m f", m=M), i["relT"].rearrange("m j d -> j m d")),
                             (o1, i["outW"][0:D, :]), (o2, i["outW"][D:2 * D, :]), (ob, i["outb"]),
                             (gb, i["gb"].partition_broadcast(P))):
                sp.dma_start(dst, src).then_inc(wld, 16)

            def load(c):
                sp.wait_ge(mx, c + 1)
                hold(sp)
                sp.dma_start(h, d["h"][bass.ds(c * CN, CN), :].rearrange("(b p) f -> p b f", p=P)).then_inc(hl, 16)
                sp.dma_start(x1, d["x1"][bass.ds(c * CN, CN), :].rearrange("(b p) f -> p b f", p=P)).then_inc(xl, 16)

            load(0)
            with sp.Fori(0, NCH - 1) as c:
                load(c + 1)
                sp.wait_ge(ln, c + 1)
                hold(sp)
                sp.dma_start(out[bass.ds(c * CN, CN), :].rearrange("(b p) f -> p b f", p=P), y).then_inc(ost, 16)
            sp.wait_ge(ln, NCH)
            sp.dma_start(out[(NCH - 1) * CN:NP, :].rearrange("(b p) f -> p b f", p=P), y).then_inc(ost, 16)
            sp.wait_ge(ost, 16 * NCH + 16)

        @block.tensor
        def _(pe):
            pe.wait_ge(wld, 6 * 16)
            for k in range(M):
                nc.tensor.matmul(bank[0][:, 0:P], att[:, k * P:(k + 1) * P], o1, start=(k == 0), stop=(k == M - 1))
            for m in range(M):
                last = nc.tensor.matmul(bank[0][:, (1 + m) * P:(2 + m) * P], rel[:, m * P:(m + 1) * P], o2,
                                        start=True, stop=True)
            last.then_inc(wp, 1)
            pe.wait_ge(wc, 1 + M)

            def product(c):
                pe.wait_ge(sr, c + 1)
                for s in range(2):
                    for k in range(1 + M):
                        last = nc.tensor.matmul(bank[1 + s][:, 0:H], w[k], acc[:, k, bass.ds(c * CN + s * H, H)],
                                                start=(k == 0), stop=(k == M))
                last.then_inc(su, 1)

            def turn(c):
                pe.wait_ge(sr, c + 2)
                pe.wait_ge(su_v, c + 1)
                for s, (a, z) in enumerate(HALVES):
                    for k in range(a, z):
                        last = nc.tensor.transpose(bank[3 + s][:, (k - a) * P:(k - a + 1) * P], u[:, k * P:(k + 1) * P],
                                                   ident[:, :])
                last.then_inc(sT, 1)

            pe.wait_ge(sj, 1)
            product(0)
            with pe.Fori(0, NCH - 1) as c:
                product(c + 1)
                turn(c)
            turn(NCH - 1)

        @block.scalar
        def _(act):
            act.wait_ge(wld, 6 * 16)
            nc.scalar.activation(gate, t["gate_n"][:, :], ACT.Sigmoid, bias=gb).then_inc(gs, 1)
            act.wait_ge(wp, 1)
            for k in range(1 + M):
                nc.scalar.activation(w[k], bank[0][:, k * P:(k + 1) * P], ACT.Copy, scale=1.0 / 3.0).then_inc(wc, 1)
            act.wait_ge(eps_s, 1)

            def relu(c):
                act.wait_ge(su, c + 1)
                act.wait_ge(sT, c + 1)
                nc.scalar.activation(u[:, 0:H], bank[1][:, 0:H], ACT.Relu, bias=ob)
                nc.scalar.activation(u[:, H:CN], bank[2][:, 0:H], ACT.Relu, bias=ob).then_inc(sr, 1)

            def square_root(c):
                act.wait_ge(ask, c + 1)
                nc.scalar.activation(std, std, ACT.Sqrt, bias=eps, scale=1.0 / D).then_inc(root, 1)

            relu(0)
            with act.Fori(0, NCH - 1) as c:
                relu(c + 1)
                square_root(c)
            square_root(NCH - 1)

        @block.gpsimd
        def _(pool):
            for n, (s, per) in enumerate([(mx, 1), (sr, 1), (sT, 1), (su_v, 1), (ost, 16)]):
                nc.gpsimd.memset(start[:, n:n + 1], 0.0).then_inc(s, per)
            pool.wait_ge(cf, 1)
            with pool.Fori(0, NCH) as c:
                cc = Count(pool, mxc, c * 2)
                pool.wait_ge(hl, c * 16 + 16)
                pool.wait_ge(xl, c * 16 + 16)
                pool.wait_ge(su_v, c + 1)
                cc.add(nc.gpsimd.tensor_tensor(rest, h, chh[:, bass.ds(c * CB, CB)].unsqueeze(2)
                                               .to_broadcast([P, CB, P]), ALU.mult))
                cc.add(nc.gpsimd.tensor_tensor(x1, x1, cx[:, bass.ds(c * CB, CB)].unsqueeze(2)
                                               .to_broadcast([P, CB, P]), ALU.mult))
                cc.wait()
                nc.gpsimd.tensor_tensor(rest, rest, x1, ALU.add).then_inc(mx, 1)

        @block.vector
        def _(dve):
            nc.vector.memset(eps, EPS).then_inc(eps_s, 1)
            nc.vector.tensor_tensor(acc[:, 0, :], acc[:, 0, :], t["hT"][:, :], ALU.add).then_inc(sj, 1)
            dve.wait_ge(gs, 1)
            c0 = Count(dve, ch)
            c0.link(nc.vector.tensor_tensor(cu, gate, t["has_n"][:, :], ALU.mult))
            c0.add(nc.vector.tensor_tensor(chh, gate, cu, ALU.subtract))
            c0.add(nc.vector.tensor_scalar(cx, gate, -1.0, 2.0, ALU.mult, ALU.add))
            c0.wait()
            nc.vector.memset(mean, 0.0).then_inc(cf, 1)
            PRE, PER = 3, 2 + 5
            with dve.Fori(0, NCH) as it:
                c = Count(dve, ch, it * PER + PRE)
                dve.wait_ge(sT, it + 2)
                dve.wait_ge(mx, it + 2)
                for s, (a, z) in enumerate(HALVES):
                    c.add(nc.vector.tensor_tensor(v[:, a:z, :], blocks_view(bank[3 + s], a, z),
                                                  cu[:, bass.ds(it * CB + a, z - a)].unsqueeze(2)
                                                  .to_broadcast([P, z - a, P]), ALU.mult))
                c.wait()
                nc.vector.tensor_tensor(v, v, rest, ALU.add).then_inc(su_v, 1)
                dve.wait_ge(su_v, it + 2)
                dve.wait_ge(ost, it * 16 + 16)
                layer_norm(c, ask, root, it + 1, [((0, CB), v)], mean, cen, sq, std, y).then_inc(ln, 1)
                assert c.n == PER


def build(nc, i, out):
    def dram(name, shape, dt=F32):
        return nc.dram_tensor("d_" + name, shape, dt).ap()

    d = dict(tiles=dram("tiles", [TC * P, TW]), B=dram("src_product", [NP, P]),
             valid=dram("valid", [JP * P]), keep=dram("keep", [JP * P]), stop=dram("stop", [JP * P]),
             reset=dram("reset", [JP * P], BF16), w3=dram("w3", [3, JP * P], BF16), ww9=dram("ww9", [9, P], BF16),
             base=dram("base", [JP], I32), gates=dram("gates", [JP, M * P]),
             flat=dram("flat", [M, JP * P]), wflat=dram("wflat", [M, JP * P]),
             x1=dram("x1", [NP, P]), h=dram("h", [NP, P]), hsp=dram("rows", [JP // GJ, P, GJ * P]))
    with ExitStack() as ctx:
        t = tensors(nc, ctx)
        phase_tables(nc, t, i, d)
        phase_layer0(nc, t, i, d)
        phase_softmax(nc, t, i, d, True)
        phase_nodes0(nc, t, i, d)
        phase_scores(nc, t, i, d)
        phase_softmax(nc, t, i, d, False)
        phase_sums(nc, t, i, d)
        phase_nodes1(nc, t, i, d, out)


def kernel(x, src, dst, edge_attr_64, edge_weight, L0_gnn_Wm, L0_gnn_bm, L0_gnn_W1, L0_gnn_b1, L0_gnn_W2, L0_gnn_b2,
           L1_gnn_node_att_W, L1_gnn_rel_att_W, L1_gnn_rel_att_W1, L1_gnn_rel_att_b1, L1_gnn_rel_att_W2,
           L1_gnn_rel_att_b2, L1_gnn_node_fc_W, L1_gnn_node_fc_b, L1_gnn_edge_fc_W, L1_gnn_edge_fc_b,
           L1_gnn_out_fc_W, L1_gnn_out_fc_b, L1_gnn_gate_W, L1_gnn_gate_b):
    import numpy as np
    import concourse.bacc as bacc
    from concourse.bass_utils import run_bass_kernel_spmd

    a = lambda v: np.ascontiguousarray(v)
    f32, i32 = np.float32, np.int32
    pad = TC * P * P - E
    col, row = (lambda v: a(v).reshape(-1, 1)), (lambda v: a(v).reshape(1, -1))
    ea = np.concatenate([a(edge_attr_64), np.zeros((JP * P - E, DE), f32)])
    arrays = dict(
        dst=np.concatenate([np.full(1, -1, i32), a(dst), np.full(pad + 1, PAD_DST, i32)]),
        src=np.concatenate([a(src), np.zeros(pad, i32)]),
        w=np.concatenate([a(edge_weight), np.zeros(pad, f32)]),
        xT=a(np.concatenate([a(x), np.zeros((NP - N, D), f32)]).T),
        xrow=np.concatenate([a(x), np.zeros((NP + CN - N, D), f32)]),
        eaT=a(ea.reshape(JP // GJ, GJ * P, DE).transpose(0, 2, 1)),
        Wm=a(L0_gnn_Wm), bm=col(L0_gnn_bm), W1=a(L0_gnn_W1), b1=col(L0_gnn_b1), W2=a(L0_gnn_W2), b2v=a(L0_gnn_b2),
        weT=a(np.asarray(L1_gnn_edge_fc_W).T), be=col(L1_gnn_edge_fc_b), w1=a(L1_gnn_rel_att_W1),
        b1T=a(np.asarray(L1_gnn_rel_att_b1).T), w2T=a(np.asarray(L1_gnn_rel_att_W2).T), b2=a(L1_gnn_rel_att_b2),
        fc=a(L1_gnn_node_fc_W), fcb=col(L1_gnn_node_fc_b), fcbrow=row(L1_gnn_node_fc_b),
        attT=a(np.asarray(L1_gnn_node_att_W).transpose(0, 2, 1)),
        relT=a(np.asarray(L1_gnn_rel_att_W).transpose(0, 2, 1)),
        outW=a(L1_gnn_out_fc_W), outb=col(L1_gnn_out_fc_b), gw=a(L1_gnn_gate_W), gb=a(L1_gnn_gate_b))
    nc = bacc.Bacc("TRN2", target_bir_lowering=False, num_devices=1)
    i = {k: nc.dram_tensor(k, v.shape, mybir.dt.from_np(v.dtype), kind="ExternalInput").ap() for k, v in arrays.items()}
    out = nc.dram_tensor("out", [NP, D], F32, kind="ExternalOutput").ap()
    build(nc, i, out)
    r = run_bass_kernel_spmd(nc, [arrays], core_ids=[0])
    return r.results[0]["out"][:N]
```
